# Optimizing a Trainium2 kernel written in Bass

```python
import numpy as np
import jax
import jax.numpy as jnp

def _softmax(x, axis=-1):
    return jax.nn.softmax(x, axis=axis)

def _gelu(x):
    return jax.nn.gelu(x, approximate=True)

def _silu(x):
    return jax.nn.silu(x)

def _sigmoid(x):
    return jax.nn.sigmoid(x)

def _layernorm(x, axis=-1, eps=1e-05):
    m = jnp.mean(x, axis=axis, keepdims=True)
    v = jnp.var(x, axis=axis, keepdims=True)
    return (x - m) / jnp.sqrt(v + eps)

def _scatter_add(tgt, idx, src, axis=0):
    return tgt.at[idx].add(src)

def _segment_sum(src, seg, n):
    return jax.ops.segment_sum(src, seg, n)
kernel_name = 'mk_dlrm_tower_d1_rec_r8_bb374d'

def setup_inputs(seed: int=0):
    np.random.seed(seed)
    _w = jnp.asarray

    def _rec_inputs():
        import jax
        import jax.numpy as jnp
        _tk = jax.random.key(seed)
        dense_ctx = jax.random.normal(jax.random.fold_in(_tk, 190), (1024, 16), jnp.float32)
        ids = jnp.stack([jax.random.randint(jax.random.fold_in(_tk, 200 + f), (1024,), 0, v, jnp.int32) for f, v in enumerate([12500, 125000, 1250, 125000, 125000, 1000, 1250, 1000, 1250, 1250, 12500, 1000, 1000, 1000, 12500, 1250, 12500, 1250, 1250, 1250, 1250, 12500, 12500, 1000, 1000, 12500, 1000, 1000, 1000, 1250, 1250, 1000])], axis=1)
        tbl_0 = 0.05 * jax.random.normal(jax.random.fold_in(_tk, 500 + 0), (12500, 64), jnp.float32)
        tbl_1 = 0.05 * jax.random.normal(jax.random.fold_in(_tk, 500 + 1), (125000, 64), jnp.float32)
        tbl_2 = 0.05 * jax.random.normal(jax.random.fold_in(_tk, 500 + 2), (1250, 64), jnp.float32)
        tbl_3 = 0.05 * jax.random.normal(jax.random.fold_in(_tk, 500 + 3), (125000, 64), jnp.float32)
        tbl_4 = 0.05 * jax.random.normal(jax.random.fold_in(_tk, 500 + 4), (125000, 64), jnp.float32)
        tbl_5 = 0.05 * jax.random.normal(jax.random.fold_in(_tk, 500 + 5), (1000, 64), jnp.float32)
        tbl_6 = 0.05 * jax.random.normal(jax.random.fold_in(_tk, 500 + 6), (1250, 64), jnp.float32)
        tbl_7 = 0.05 * jax.random.normal(jax.random.fold_in(_tk, 500 + 7), (1000, 64), jnp.float32)
        tbl_8 = 0.05 * jax.random.normal(jax.random.fold_in(_tk, 500 + 8), (1250, 64), jnp.float32)
        tbl_9 = 0.05 * jax.random.normal(jax.random.fold_in(_tk, 500 + 9), (1250, 64), jnp.float32)
        tbl_10 = 0.05 * jax.random.normal(jax.random.fold_in(_tk, 500 + 10), (12500, 64), jnp.float32)
        tbl_11 = 0.05 * jax.random.normal(jax.random.fold_in(_tk, 500 + 11), (1000, 64), jnp.float32)
        tbl_12 = 0.05 * jax.random.normal(jax.random.fold_in(_tk, 500 + 12), (1000, 64), jnp.float32)
        tbl_13 = 0.05 * jax.random.normal(jax.random.fold_in(_tk, 500 + 13), (1000, 64), jnp.float32)
        tbl_14 = 0.05 * jax.random.normal(jax.random.fold_in(_tk, 500 + 14), (12500, 64), jnp.float32)
        tbl_15 = 0.05 * jax.random.normal(jax.random.fold_in(_tk, 500 + 15), (1250, 64), jnp.float32)
        tbl_16 = 0.05 * jax.random.normal(jax.random.fold_in(_tk, 500 + 16), (12500, 64), jnp.float32)
        tbl_17 = 0.05 * jax.random.normal(jax.random.fold_in(_tk, 500 + 17), (1250, 64), jnp.float32)
        tbl_18 = 0.05 * jax.random.normal(jax.random.fold_in(_tk, 500 + 18), (1250, 64), jnp.float32)
        tbl_19 = 0.05 * jax.random.normal(jax.random.fold_in(_tk, 500 + 19), (1250, 64), jnp.float32)
        tbl_20 = 0.05 * jax.random.normal(jax.random.fold_in(_tk, 500 + 20), (1250, 64), jnp.float32)
        tbl_21 = 0.05 * jax.random.normal(jax.random.fold_in(_tk, 500 + 21), (12500, 64), jnp.float32)
        tbl_22 = 0.05 * jax.random.normal(jax.random.fold_in(_tk, 500 + 22), (12500, 64), jnp.float32)
        tbl_23 = 0.05 * jax.random.normal(jax.random.fold_in(_tk, 500 + 23), (1000, 64), jnp.float32)
        tbl_24 = 0.05 * jax.random.normal(jax.random.fold_in(_tk, 500 + 24), (1000, 64), jnp.float32)
        tbl_25 = 0.05 * jax.random.normal(jax.random.fold_in(_tk, 500 + 25), (12500, 64), jnp.float32)
        tbl_26 = 0.05 * jax.random.normal(jax.random.fold_in(_tk, 500 + 26), (1000, 64), jnp.float32)
        tbl_27 = 0.05 * jax.random.normal(jax.random.fold_in(_tk, 500 + 27), (1000, 64), jnp.float32)
        tbl_28 = 0.05 * jax.random.normal(jax.random.fold_in(_tk, 500 + 28), (1000, 64), jnp.float32)
        tbl_29 = 0.05 * jax.random.normal(jax.random.fold_in(_tk, 500 + 29), (1250, 64), jnp.float32)
        tbl_30 = 0.05 * jax.random.normal(jax.random.fold_in(_tk, 500 + 30), (1250, 64), jnp.float32)
        tbl_31 = 0.05 * jax.random.normal(jax.random.fold_in(_tk, 500 + 31), (1000, 64), jnp.float32)
        _rk = jax.random.fold_in(_tk, 7)
        W_top1 = 0.0693375 * jax.random.normal(jax.random.fold_in(_tk, 801), (208, 512), jnp.float32)
        W_top2 = 0.0441942 * jax.random.normal(jax.random.fold_in(_tk, 802), (512, 256), jnp.float32)
        W_top3 = 0.0625 * jax.random.normal(jax.random.fold_in(_tk, 803), (256, 1), jnp.float32)
        b_top1 = jnp.zeros((512,), jnp.float32)
        b_top2 = jnp.zeros((256,), jnp.float32)
        return (dense_ctx, ids, tbl_0, tbl_1, tbl_2, tbl_3, tbl_4, tbl_5, tbl_6, tbl_7, tbl_8, tbl_9, tbl_10, tbl_11, tbl_12, tbl_13, tbl_14, tbl_15, tbl_16, tbl_17, tbl_18, tbl_19, tbl_20, tbl_21, tbl_22, tbl_23, tbl_24, tbl_25, tbl_26, tbl_27, tbl_28, tbl_29, tbl_30, tbl_31, W_top1, b_top1, W_top2, b_top2, W_top3)
    dense_ctx, ids, tbl_0, tbl_1, tbl_2, tbl_3, tbl_4, tbl_5, tbl_6, tbl_7, tbl_8, tbl_9, tbl_10, tbl_11, tbl_12, tbl_13, tbl_14, tbl_15, tbl_16, tbl_17, tbl_18, tbl_19, tbl_20, tbl_21, tbl_22, tbl_23, tbl_24, tbl_25, tbl_26, tbl_27, tbl_28, tbl_29, tbl_30, tbl_31, W_top1, b_top1, W_top2, b_top2, W_top3 = _rec_inputs()

    def _L0_rec_setup():
        import jax, jax.numpy as jnp
        import numpy as np
        FIELD = 32
        DIM = 64
        LAYER_SIZE = (128, 128)

        def _cin(x, weights, biases):
            B, F, D = x.shape
            hidden = x
            finals = []
            n_layers = len(weights)
            for i, (w, b) in enumerate(zip(weights, biases)):
                size = w.shape[0]
                z = jnp.einsum('bhd,bfd->bhfd', hidden, x).reshape(B, hidden.shape[1] * F, D)
                y = jnp.einsum('bcd,oc->bod', z, w) + b[None, :, None]
                y = jax.nn.relu(y)
                if i != n_layers - 1:
                    hidden, direct = (y[:, :size // 2, :], y[:, size // 2:, :])
                else:
                    direct = y
                finals.append(direct)
            return jnp.concatenate(finals, axis=1).sum(-1)
        key = jax.random.key(seed)
        ks = jax.random.split(key, 5)
        B = 512
        x = jax.random.normal(ks[0], (B, FIELD, DIM), dtype=jnp.float32)
        field_nums = [FIELD]
        params = {}
        for i, size in enumerate(LAYER_SIZE):
            in_ch = field_nums[-1] * field_nums[0]
            fan = 1.0 / np.sqrt(in_ch)
            params[f'w{i}'] = jax.random.uniform(ks[1 + 2 * i % 4], (size, in_ch), minval=-fan, maxval=fan, dtype=jnp.float32)
            params[f'b{i}'] = jax.random.uniform(ks[2 + 2 * i % 4], (size,), minval=-fan, maxval=fan, dtype=jnp.float32)
            field_nums.append(size // 2)
        return {'cin_inputs': x, 'w0': params['w0'], 'b0': params['b0'], 'w1': params['w1'], 'b1': params['b1']}
    _L0_rec_all = _L0_rec_setup()
    _L0_rec_in = {k: v for k, v in _L0_rec_all.items() if k in ('w0', 'b0', 'w1', 'b1')}
    del _L0_rec_all
    return {'dense_ctx': dense_ctx, 'ids': ids, 'tbl_0': tbl_0, 'tbl_1': tbl_1, 'tbl_2': tbl_2, 'tbl_3': tbl_3, 'tbl_4': tbl_4, 'tbl_5': tbl_5, 'tbl_6': tbl_6, 'tbl_7': tbl_7, 'tbl_8': tbl_8, 'tbl_9': tbl_9, 'tbl_10': tbl_10, 'tbl_11': tbl_11, 'tbl_12': tbl_12, 'tbl_13': tbl_13, 'tbl_14': tbl_14, 'tbl_15': tbl_15, 'tbl_16': tbl_16, 'tbl_17': tbl_17, 'tbl_18': tbl_18, 'tbl_19': tbl_19, 'tbl_20': tbl_20, 'tbl_21': tbl_21, 'tbl_22': tbl_22, 'tbl_23': tbl_23, 'tbl_24': tbl_24, 'tbl_25': tbl_25, 'tbl_26': tbl_26, 'tbl_27': tbl_27, 'tbl_28': tbl_28, 'tbl_29': tbl_29, 'tbl_30': tbl_30, 'tbl_31': tbl_31, 'W_top1': W_top1, 'b_top1': b_top1, 'W_top2': W_top2, 'b_top2': b_top2, 'W_top3': W_top3, 'L0_rec_w0': _L0_rec_in['w0'], 'L0_rec_b0': _L0_rec_in['b0'], 'L0_rec_w1': _L0_rec_in['w1'], 'L0_rec_b1': _L0_rec_in['b1']}

def reference(dense_ctx, ids, tbl_0, tbl_1, tbl_2, tbl_3, tbl_4, tbl_5, tbl_6, tbl_7, tbl_8, tbl_9, tbl_10, tbl_11, tbl_12, tbl_13, tbl_14, tbl_15, tbl_16, tbl_17, tbl_18, tbl_19, tbl_20, tbl_21, tbl_22, tbl_23, tbl_24, tbl_25, tbl_26, tbl_27, tbl_28, tbl_29, tbl_30, tbl_31, W_top1, b_top1, W_top2, b_top2, W_top3, L0_rec_w0, L0_rec_b0, L0_rec_w1, L0_rec_b1):
    import jax
    import jax.numpy as jnp

    def _L0_rec_ref(cin_inputs, w0, b0, w1, b1):
        import jax, jax.numpy as jnp
        import numpy as np
        FIELD = 32
        DIM = 64
        LAYER_SIZE = (128, 128)

        def _cin(x, weights, biases):
            B, F, D = x.shape
            hidden = x
            finals = []
            n_layers = len(weights)
            for i, (w, b) in enumerate(zip(weights, biases)):
                size = w.shape[0]
                z = jnp.einsum('bhd,bfd->bhfd', hidden, x).reshape(B, hidden.shape[1] * F, D)
                y = jnp.einsum('bcd,oc->bod', z, w) + b[None, :, None]
                y = jax.nn.relu(y)
                if i != n_layers - 1:
                    hidden, direct = (y[:, :size // 2, :], y[:, size // 2:, :])
                else:
                    direct = y
                finals.append(direct)
            return jnp.concatenate(finals, axis=1).sum(-1)
        return _cin(cin_inputs, [w0, w1], [b0, b1])
    e = jnp.stack([tbl_0[ids[:, 0]], tbl_1[ids[:, 1]], tbl_2[ids[:, 2]], tbl_3[ids[:, 3]], tbl_4[ids[:, 4]], tbl_5[ids[:, 5]], tbl_6[ids[:, 6]], tbl_7[ids[:, 7]], tbl_8[ids[:, 8]], tbl_9[ids[:, 9]], tbl_10[ids[:, 10]], tbl_11[ids[:, 11]], tbl_12[ids[:, 12]], tbl_13[ids[:, 13]], tbl_14[ids[:, 14]], tbl_15[ids[:, 15]], tbl_16[ids[:, 16]], tbl_17[ids[:, 17]], tbl_18[ids[:, 18]], tbl_19[ids[:, 19]], tbl_20[ids[:, 20]], tbl_21[ids[:, 21]], tbl_22[ids[:, 22]], tbl_23[ids[:, 23]], tbl_24[ids[:, 24]], tbl_25[ids[:, 25]], tbl_26[ids[:, 26]], tbl_27[ids[:, 27]], tbl_28[ids[:, 28]], tbl_29[ids[:, 29]], tbl_30[ids[:, 30]], tbl_31[ids[:, 31]]], axis=1)
    z = _L0_rec_ref(e, L0_rec_w0, L0_rec_b0, L0_rec_w1, L0_rec_b1)
    z = z.reshape(z.shape[0], -1)
    h = jnp.concatenate([z, dense_ctx], axis=1)
    h = jnp.maximum(h @ W_top1 + b_top1, 0.0)
    h = jnp.maximum(h @ W_top2 + b_top2, 0.0)
    y = h @ W_top3
    return y

_drawn_inputs = setup_inputs


def setup_inputs(seed=0):
    import zlib

    import numpy as np

    out = dict(_drawn_inputs(seed))
    spreads = {'b_top1': (0.0, 0.415), 'b_top2': (0.0, 0.1)}
    factors = {'tbl_0': 8.0,
     'tbl_1': 8.0,
     'tbl_2': 8.0,
     'tbl_3': 8.0,
     'tbl_4': 8.0,
     'tbl_5': 8.0,
     'tbl_6': 8.0,
     'tbl_7': 8.0,
     'tbl_8': 8.0,
     'tbl_9': 8.0,
     'tbl_10': 8.0,
     'tbl_11': 8.0,
     'tbl_12': 8.0,
     'tbl_13': 8.0,
     'tbl_14': 8.0,
     'tbl_15': 8.0,
     'tbl_16': 8.0,
     'tbl_17': 8.0,
     'tbl_18': 8.0,
     'tbl_19': 8.0,
     'tbl_20': 8.0,
     'tbl_21': 8.0,
     'tbl_22': 8.0,
     'tbl_23': 8.0,
     'tbl_24': 8.0,
     'tbl_25': 8.0,
     'tbl_26': 8.0,
     'tbl_27': 8.0,
     'tbl_28': 8.0,
     'tbl_29': 8.0,
     'tbl_30': 8.0,
     'tbl_31': 8.0,
     'L0_rec_w1': 6.341}
    for name, (base, spread) in spreads.items():
        noise = np.random.default_rng([zlib.crc32(name.encode()), seed]).standard_normal(out[name].shape)
        drawn = base * np.exp(spread * noise) if base else spread * noise
        out[name] = jnp.asarray(drawn.astype(out[name].dtype))
    for name, factor in factors.items():
        out[name] = (out[name] * factor).astype(out[name].dtype)
    return out
```

```python
from contextlib import ExitStack

import numpy as np

import concourse.bass as bass
from concourse import mybir

F32 = mybir.dt.float32
I32 = mybir.dt.int32
ALU = mybir.AluOpType
ACT = mybir.ActivationFunctionType
AX_X = mybir.AxisListType.X

P = 128
FIELDS = 32
DIM = 64
HID = 64
OUT = 128
N = 512
SPT = N // DIM
PAIR = 2 * N
ROT = 4
STEP = 4
HALF = 16
LEFT = 16
W2 = 2 * FIELDS
U = {(0, 0): 0, (0, 1): 31, (1, 0): 30, (1, 1): 31}
TPB = 4


def build(nc, dense, ids, tables, W_top1, b_top1, W_top2, b_top2, W_top3, w0, b0, w1, b1, out):
    B = ids.shape[0]
    TILES = B // SPT
    PAIRS = TILES // 2
    BODIES = TILES // TPB
    GT = B // P
    PPG = P // (2 * SPT)
    DENSE = dense.shape[1]
    H1, H2 = W_top1.shape[1], W_top2.shape[1]
    M1, M2 = H1 // P, H2 // P
    assert FIELDS * 2 == HID == DIM and len(tables) == FIELDS and PPG % 2 == 0 and GT % 2 == 0

    x_dram = nc.dram_tensor("x_rows", (2 * FIELDS, B * DIM), F32, kind="Internal").ap()
    ROW = B * DIM

    with ExitStack() as ctx:
        def sb(name, shape, dt=F32):
            return ctx.enter_context(nc.sbuf_tensor(name, shape, dt))

        def ps(name, shape):
            return ctx.enter_context(nc.psum_tensor(name, shape, F32))

        def sem(name):
            return ctx.enter_context(nc.semaphore(name))

        xrot = sb("xrot", [P, 2, ROT, PAIR])
        xoth = sb("xoth", [P, 2, PAIR])
        xleft = sb("xleft", [LEFT, 2, PAIR])
        hid = sb("hid", [P, 2, ROT, N])
        z0 = sb("z0", [P, ROT, N])
        zl = sb("zl", [P, N])
        z1 = [sb(f"z1_{i}", [P, ROT, N]) for i in range(ROT)]
        direct = sb("direct", [P, 2, N])
        last = sb("last", [P, 2, N])
        sum0 = sb("sum0", [P, B])
        sum1 = sb("sum1", [P, B])
        rows = sb("rows", [P, 2, FIELDS, DIM])
        idt = sb("idt", [P, 2, FIELDS], I32)
        w0T = sb("w0T", [P, ROT + 1, OUT])
        w1T = sb("w1T", [P, ROT, ROT, OUT])
        ident = sb("ident", [P, P])
        bias0 = sb("bias0", [P, 1])
        bias1 = sb("bias1", [P, 1])
        biasA = sb("biasA", [P, M1])
        biasB = sb("biasB", [P, M2])
        wA = sb("wA", [P, 2, H1])
        wB = sb("wB", [P, M1, H2])
        wC = sb("wC", [P, M2])
        dn = sb("dn", [P, B // P, DENSE])
        yrow = sb("yrow", [1, B])
        w1n = z1[0][:, :, :].rearrange("p a b -> p (a b)")
        w0n = z1[1][:, 0:2, :].rearrange("p a b -> p (a b)")
        fold = z1[1][:, 2:4, :].rearrange("p a b -> p (a b)")[:, 0:(ROT + 1) * P].rearrange(
            "p (k r) -> p k r", k=ROT + 1)
        w0d = xrot[:, 0, :, :].rearrange("p a b -> p (a b)")
        w1d_t = sb("w1d_t", [P, (HID + ROT) * W2])
        walks = z1[2][:, :, :].rearrange("p i (j r) -> p i j r", j=ROT)
        hA = [z1[m][:, 0:B // N, :] for m in range(M1)]
        hB = [z0[:, (B // N) * m:(B // N) * (m + 1), :] for m in range(M2)]

        y0 = ps("y0", [P, 2, N])
        y1 = ps("y1", [P, 2, N])
        pt = ps("pt", [P, 4, N])

        weight_banks = [pt[:, 2, :], pt[:, 3, :], y0[:, 0, :], y0[:, 1, :], y1[:, 0, :], y1[:, 1, :]]

        ident_zero = sem("ident_zero")
        ident_ready = sem("ident_ready")
        ids_in = sem("ids_in")
        ids_seen = sem("ids_seen")
        gathered = [sem(f"gathered{s}") for s in range(2)]
        x_written = [sem(f"x_written{s}") for s in range(2)]
        w_in = sem("w_in")
        top_in = sem("top_in")
        zeroed = sem("zeroed")
        w0_repeated = sem("w0_repeated")
        w1_repeated = sem("w1_repeated")
        w1_walked = sem("w1_walked")
        w0_folded = sem("w0_folded")
        w_turned = sem("w_turned")
        w_ready = sem("w_ready")
        dense_turned = sem("dense_turned")
        dense_ready = sem("dense_ready")
        x_in = [sem(f"x_in{s}") for s in range(2)]
        hid_in = [[None] + [sem(f"hid_in{s}_{i}") for i in range(1, ROT)] for s in range(2)]
        z0_ready = sem("z0_ready")
        l0_done = sem("l0_done")
        hid_ready = sem("hid_ready")
        direct_ready = sem("direct_ready")
        direct_summed = sem("direct_summed")
        z1_ready = sem("z1_ready")
        l1_blocks = sem("l1_blocks")
        last_ready = sem("last_ready")
        last_summed = sem("last_summed")
        hA_mm = sem("hA_mm")
        hA_ready = sem("hA_ready")
        hB_mm = sem("hB_mm")
        hB_ready = sem("hB_ready")
        y_mm = sem("y_mm")
        y_ready = sem("y_ready")
        y_out = sem("y_out")

        X_LOADS = 7
        ids_v = ids
        block = ctx.enter_context(nc.Block())

        def at_least(eng, s, value):
            if not isinstance(value, int) or value > 0:
                eng.wait_ge(s, value)

        def view(ap, offset, dims):
            return bass.AP(ap.tensor, ap.offset + offset, [list(ap.ap[0])] + [list(d) for d in dims])

        @block.gpsimd
        def _(pool):
            nc.gpsimd.memset(ident[:], 0.0).then_inc(ident_zero, 1)
            pool.wait_ge(ident_zero, 1)
            nc.gpsimd.affine_select(out=ident[:], in_=ident[:], compare_op=ALU.not_equal, fill=1.0, base=0,
                                    pattern=[[-1, P]], channel_multiplier=1).then_inc(ident_ready, 1)

            def gather(g, s, first):
                if not first:
                    pool.wait_ge(x_written[s], (g - s) // 2 * 32 if isinstance(g, int) else (g - s) * 16)
                pool.dma_start(idt[:, s, :], ids_v[bass.ds(g * P, P), :]).then_inc(ids_in, 16)
                pool.wait_ge(ids_in, (g + 1) * 16)
                pool.sem_inc(ids_seen, 1)
                for f in range(FIELDS):
                    pool.indirect_dma_start(
                        out=rows[:, s, f, :], out_offset=None, in_=tables[f],
                        in_offset=bass.IndirectOffsetOnAxis(ap=idt[:, s, f:f + 1], axis=0),
                    ).then_inc(gathered[s], 16)
                pool.wait_ge(gathered[s], (g - s) * (8 * FIELDS) + 16 * FIELDS)
                for copy in range(2):
                    dst = bass.AP(x_dram.tensor, x_dram.offset + copy * FIELDS * ROW + g * (P * DIM),
                                  [[DIM, P], [ROW, FIELDS], [1, DIM]])
                    pool.dma_start(dst, rows[:, s, :, :]).then_inc(x_written[s], 16)

            gather(0, 0, True)
            gather(1, 1, True)
            with pool.Fori(1, GT // 2) as h:
                for s in range(2):
                    gather(2 * h + s, s, False)
            pool.wait_ge(x_written[0], GT * 16)
            pool.wait_ge(x_written[1], GT * 16)

        @block.sync
        def _(sp):
            sp.dma_start(w0n, w0).then_inc(w_in, 16)
            sp.dma_start(w1n, w1).then_inc(w_in, 16)
            sp.dma_start(bias0[:], b0.rearrange("(p a) -> p a", a=1)).then_inc(w_in, 16)
            sp.dma_start(bias1[:], b1.rearrange("(p a) -> p a", a=1)).then_inc(w_in, 16)

            def load_x(pair, s):
                base = x_dram.offset + pair * PAIR
                for c in range(2):
                    for h in range(2):
                        g = 64 * c + 32 * h
                        src = bass.AP(x_dram.tensor, base + HALF * c * ROW,
                                      [[ROW, FIELDS], [STEP * ROW, ROT], [1, PAIR]])
                        sp.dma_start(xrot[g:g + 32, s, :, :], src).then_inc(x_in[s], 16)
                for c in range(2):
                    d = U[c, 1] - U[c, 0]
                    src = bass.AP(x_dram.tensor, base + U[c, 0] * ROW,
                                  [[d * ROW, 2], [ROW, FIELDS], [1, PAIR]])
                    sp.dma_start(xoth[64 * c:64 * c + 64, s, :], src).then_inc(x_in[s], 16)
                src = bass.AP(x_dram.tensor, base + HALF * ROW, [[ROW, LEFT], [1, PAIR]])
                sp.dma_start(xleft[:, s, :], src).then_inc(x_in[s], 16)

            def rotate_hidden(t, s):
                sp.wait_ge(hid_ready, 2 * t + 2)
                for i in range(1, ROT):
                    for c in range(2):
                        sp.dma_start(hid[64 * c:64 * c + 64, s, i, :],
                                     hid[i:i + 64, s, 0, :]).then_inc(hid_in[s][i], 16)

            sp.dma_start(dn[:], dense.rearrange("(q p) c -> p q c", p=P)).then_inc(top_in, 16)
            sp.dma_start(wA[64:128, 0, :], W_top1[0:HID, :]).then_inc(top_in, 16)
            sp.wait_ge(zeroed, 4)
            sp.dma_start(wA[0:DENSE, 0, :], W_top1[HID + OUT:HID + OUT + DENSE, :]).then_inc(top_in, 16)
            sp.dma_start(wA[:, 1, :], W_top1[HID:HID + OUT, :]).then_inc(top_in, 16)
            sp.dma_start(wB[:], W_top2.rearrange("(m p) n -> p m n", p=P)).then_inc(top_in, 16)
            with nc.allow_non_contiguous_dma(reason="a few hundred bias and weight values"):
                sp.dma_start(wC[:], W_top3.rearrange("(m p) a -> p (m a)", p=P)).then_inc(top_in, 16)
                sp.dma_start(biasA[:], b_top1.rearrange("(m p) -> p m", p=P)).then_inc(top_in, 16)
                sp.dma_start(biasB[:], b_top2.rearrange("(m p) -> p m", p=P)).then_inc(top_in, 16)
            sp.wait_ge(x_written[0], 32)
            sp.wait_ge(w0_folded, 6)
            load_x(0, 0)
            load_x(1, 1)
            rotate_hidden(0, 0)

            def body(k, more, gslot=None, gcount=None):
                for q in range(TPB):
                    t = k * TPB + q
                    if more or q < TPB - 1:
                        rotate_hidden(t + 1, (q + 1) % 2)
                    if more and q % 2 == 1:
                        sp.wait_ge(z1_ready, (t + 1) * ROT)
                        load_x(k * 2 + q // 2 + 2, q // 2)

            BPG = PPG // 2
            for j in range(BPG - 1):
                body(j, True)
            with sp.Fori(1, GT // 2) as gg:
                for s in range(2):
                    g = 2 * gg + (s - 1)
                    sp.wait_ge(x_written[(s - 1) % 2], gg * 32 if s == 0 else gg * 32 + 32)
                    for j in range(BPG):
                        body(g * BPG + (j - 1), True)
            g = GT - 1
            sp.wait_ge(x_written[g % 2], GT * 16)
            for j in range(BPG):
                body(g * BPG + j - 1, True)
            body(BODIES - 1, False)
            sp.wait_ge(y_ready, B // N)
            sp.dma_start(out.rearrange("b a -> a b"), yrow[0:1, :]).then_inc(y_out, 16)
            sp.wait_ge(y_out, 16)

        @block.scalar
        def _(act):
            for n in range(6):
                act.wait_ge(w_turned, n + 1)
                if n < ROT:
                    src, dst = weight_banks[n + 2], w1T[:, n, :, :]
                    nc.scalar.activation(dst, src.rearrange("p (a b) -> p a b", a=ROT), ACT.Copy).then_inc(w_ready, 1)
                elif n == ROT:
                    nc.scalar.activation(w0T[:, 0:ROT, :], weight_banks[0].rearrange("p (a b) -> p a b", a=ROT),
                                         ACT.Copy).then_inc(w_ready, 1)
                else:
                    nc.scalar.activation(w0T[:, ROT, :], weight_banks[1][:, 0:OUT], ACT.Copy).then_inc(w_ready, 1)
            act.wait_ge(w_in, 64)
            act.wait_ge(zeroed, 4)
            act.wait_ge(dense_turned, 1)
            nc.scalar.activation(sum0[0:DENSE, :], pt[0:DENSE, 0:B // N, :].rearrange("p a b -> p (a b)"),
                                 ACT.Copy).then_inc(dense_ready, 1)

            def layer0_out(t, s):
                act.wait_ge(l0_done, t + 1)
                at_least(act, z1_ready, (t - 1) * ROT)
                for c in range(2):
                    nc.scalar.activation(hid[64 * c:64 * c + 64, s, 0, :], y0[0:HID, s, :], ACT.Relu,
                                         bias=bias0[0:HID, :]).then_inc(hid_ready, 1)
                at_least(act, direct_summed, t - 1)
                nc.scalar.activation(direct[HID:OUT, s, :], y0[HID:OUT, s, :], ACT.Relu,
                                     bias=bias0[HID:OUT, :]).then_inc(direct_ready, 1)

            def layer1_out(t, s):
                act.wait_ge(l1_blocks, (t + 1) * ROT)
                at_least(act, last_summed, t - 1)
                nc.scalar.activation(last[:, s, :], y1[:, s, :], ACT.Relu,
                                     bias=bias1[:]).then_inc(last_ready, 1)

            def body(k, more):
                for q in range(TPB):
                    t = k * TPB + q
                    if more or q < TPB - 1:
                        layer0_out(t + 1, (q + 1) % 2)
                    layer1_out(t, q % 2)

            layer0_out(0, 0)
            body(0, True)
            with act.Fori(1, BODIES - 1) as k:
                body(k, True)
            body(BODIES - 1, False)

            act.wait_ge(top_in, 8 * 16)
            for m in range(M1):
                for b in range(B // N):
                    act.wait_ge(hA_mm, (B // N) * m + b + 1)
                    nc.scalar.activation(hA[m][:, b, :], pt[:, (B // N) * (m % 2) + b, :], ACT.Relu,
                                         bias=biasA[:, m:m + 1]).then_inc(hA_ready, 1)
            for m in range(M2):
                for b in range(B // N):
                    act.wait_ge(hB_mm, (B // N) * m + b + 1)
                    nc.scalar.activation(hB[m][:, b, :], y0[:, b, :] if m == 0 else y1[:, b, :], ACT.Relu,
                                         bias=biasB[:, m:m + 1]).then_inc(hB_ready, 1)
            for b in range(B // N):
                act.wait_ge(y_mm, b + 1)
                nc.scalar.activation(yrow[0:1, b * N:(b + 1) * N], pt[0:1, b, :], ACT.Copy).then_inc(y_ready, 1)

        @block.vector
        def _(dve):
            nc.vector.memset(zl[:], 0.0).then_inc(zeroed, 1)
            nc.vector.memset(sum0[:], 0.0).then_inc(zeroed, 1)
            nc.vector.memset(wA[0:64, 0, :], 0.0).then_inc(zeroed, 1)
            nc.vector.memset(fold[:, ROT, :], 0.0).then_inc(zeroed, 1)
            dve.wait_ge(w_in, 64)
            w0v = w0n.rearrange("p (h f) -> p h f", h=FIELDS)
            w0dv = w0d.rearrange("p (h f) -> p h f", h=W2)
            for a in range(2):
                for b in range(2):
                    nc.vector.tensor_copy(w0dv[:, FIELDS * a:FIELDS * (a + 1), FIELDS * b:FIELDS * (b + 1)],
                                          w0v).then_inc(w0_repeated, 1)
            w1v = w1n.rearrange("p (h f) -> p h f", h=HID)
            w1dv = w1d_t[:, :].rearrange("p (h f) -> p h f", f=W2)
            for b in range(2):
                nc.vector.tensor_copy(w1dv[:, 0:HID, FIELDS * b:FIELDS * (b + 1)], w1v).then_inc(w1_repeated, 1)
                nc.vector.tensor_copy(w1dv[:, HID:HID + ROT, FIELDS * b:FIELDS * (b + 1)],
                                      w1v[:, 0:ROT, :]).then_inc(w1_repeated, 1)
            dve.wait_ge(w1_repeated, 4)
            for i in range(ROT):
                for c in range(2):
                    nc.vector.tensor_copy(
                        walks[:, i, :, 64 * c:64 * c + 64].rearrange("p j (h q) -> p j h q", h=2),
                        view(w1d_t[:, :], i * W2 + HALF * c,
                             [[STEP, ROT], [FIELDS * W2, 2], [W2 + 1, FIELDS]])).then_inc(w1_walked, 1)
            dve.wait_ge(w0_repeated, 4)
            dve.wait_ge(zeroed, 4)
            for c in range(2):
                for h in range(2):
                    u = U[c, h]
                    nc.vector.tensor_tensor(
                        fold[:, 0:ROT, 64 * c + 32 * h:64 * c + 32 * h + 32],
                        view(w0d, HALF * c * W2 + u, [[STEP * W2, ROT], [W2 + 1, FIELDS]]),
                        view(w0d, u * W2 + HALF * c, [[STEP, ROT], [W2 + 1, FIELDS]]),
                        ALU.add).then_inc(w0_folded, 1)
            nc.vector.tensor_tensor(fold[:, ROT, 0:LEFT], view(w0d, HALF, [[W2 + 1, LEFT]]),
                                    view(w0d, HALF * W2, [[W2 + 1, LEFT]]), ALU.add).then_inc(w0_folded, 1)
            dve.wait_ge(w0_folded, 5)
            nc.vector.tensor_copy(fold[:, 0, 0:FIELDS], view(w0d, 0, [[W2 + 1, FIELDS]])).then_inc(w0_folded, 1)

            def products0(t, s, b):
                cols = slice(b * N, (b + 1) * N)
                at_least(dve, l0_done, t)
                nc.vector.tensor_tensor(z0[:], xoth[:, s:s + 1, cols].to_broadcast([P, ROT, N]),
                                        xrot[:, s, :, cols], ALU.mult).then_inc(z0_ready, 1)
                nc.vector.tensor_tensor(zl[0:LEFT, :], xleft[:, s, cols],
                                        xrot[0:LEFT, s, 0, cols], ALU.mult).then_inc(z0_ready, 1)

            def products1(t, s, xs, b):
                cols = slice(b * N, (b + 1) * N)
                for i in range(ROT):
                    if i == 0:
                        dve.wait_ge(hid_ready, 2 * t + 2)
                    else:
                        dve.wait_ge(hid_in[s][i], (t - s) * 16 + 32)
                    at_least(dve, l1_blocks, (t - 1) * ROT + (i + 1))
                    nc.vector.tensor_tensor(z1[i][:], hid[:, s, i:i + 1, :].to_broadcast([P, ROT, N]),
                                            xrot[:, xs, :, cols], ALU.mult).then_inc(z1_ready, 1)

            def sum_direct(t, s):
                dve.wait_ge(direct_ready, t + 1)
                nc.vector.tensor_reduce(sum0[HID:OUT, bass.ds(t * SPT, SPT)],
                                        direct[HID:OUT, s, :].rearrange("p (a d) -> p a d", d=DIM),
                                        axis=AX_X, op=ALU.add).then_inc(direct_summed, 1)

            def sum_last(t, s):
                dve.wait_ge(last_ready, t + 1)
                nc.vector.tensor_reduce(sum1[:, bass.ds(t * SPT, SPT)],
                                        last[:, s, :].rearrange("p (a d) -> p a d", d=DIM),
                                        axis=AX_X, op=ALU.add).then_inc(last_summed, 1)

            def wait_x(pair_in_slot, s):
                dve.wait_ge(x_in[s], pair_in_slot)

            def body(k, first, more):
                for q in range(TPB):
                    t = k * TPB + q
                    products1(t, q % 2, q // 2, q % 2)
                    if q < 2:
                        if q == 0:
                            dve.wait_ge(x_in[1], (k + 1) * (16 * X_LOADS))
                        products0(t + 2, 1, q)
                    elif more:
                        if q == 2:
                            dve.wait_ge(x_in[0], (k + 2) * (16 * X_LOADS))
                        products0(t + 2, 0, q - 2)
                    sum_direct(t, q % 2)
                    if not (first and q == 0):
                        sum_last(t - 1, (q + 1) % 2)

            dve.wait_ge(x_in[0], 16 * X_LOADS)
            products0(0, 0, 0)
            products0(1, 0, 1)
            dve.wait_ge(w_turned, 6)
            body(0, True, True)
            with dve.Fori(1, BODIES - 1) as k:
                body(k, False, True)
            body(BODIES - 1, False, False)
            sum_last(TILES - 1, (TILES - 1) % 2)

        @block.tensor
        def _(pe):
            pe.wait_ge(ident_ready, 1)
            pe.wait_ge(w1_walked, 2 * ROT)
            for i in range(ROT):
                for j in range(ROT):
                    turned = nc.tensor.transpose(weight_banks[i + 2][:, j * OUT:(j + 1) * OUT],
                                                 walks[:, i, j, :], ident[:])
                turned.then_inc(w_turned, 1)
            pe.wait_ge(w0_folded, 6)
            for j in range(ROT):
                turned = nc.tensor.transpose(weight_banks[0][:, j * OUT:(j + 1) * OUT], fold[:, j, :], ident[:])
            turned.then_inc(w_turned, 1)
            nc.tensor.transpose(weight_banks[1][:, 0:OUT], fold[:, ROT, :], ident[:]).then_inc(w_turned, 1)
            pe.wait_ge(top_in, 8 * 16)
            for q in range(B // P):
                turned = nc.tensor.transpose(pt[0:DENSE, q // 4, (q % 4) * P:(q % 4 + 1) * P], dn[:, q, :], ident[:])
            turned.then_inc(dense_turned, 1)
            pe.wait_ge(w_ready, 6)

            def layer0(t, s):
                pe.wait_ge(z0_ready, 2 * t + 2)
                at_least(pe, direct_ready, t - 1)
                for j in range(ROT):
                    nc.tensor.matmul(y0[:, s, :], w0T[:, j, :], z0[:, j, :], start=(j == 0), stop=False)
                nc.tensor.matmul(y0[:, s, :], w0T[:, ROT, :], zl[:], start=False, stop=True).then_inc(l0_done, 1)

            def layer1(t, s):
                at_least(pe, last_ready, t - 1)
                for i in range(ROT):
                    pe.wait_ge(z1_ready, t * ROT + (i + 1))
                    for j in range(ROT):
                        mm = nc.tensor.matmul(y1[:, s, :], w1T[:, i, j, :], z1[i][:, j, :],
                                              start=(i == 0 and j == 0), stop=(i == ROT - 1 and j == ROT - 1))
                    mm.then_inc(l1_blocks, 1)

            def body(k, more):
                for q in range(TPB):
                    t = k * TPB + q
                    if more or q < TPB - 1:
                        layer0(t + 1, (q + 1) % 2)
                    layer1(t, q % 2)

            layer0(0, 0)
            body(0, True)
            with pe.Fori(1, BODIES - 1) as k:
                body(k, True)
            body(BODIES - 1, False)

            pe.wait_ge(dense_ready, 1)
            pe.wait_ge(direct_summed, TILES)
            pe.wait_ge(last_summed, TILES)
            NB = B // N
            for m in range(M1):
                for b in range(NB):
                    if m >= 2:
                        pe.wait_ge(hA_ready, NB * (m - 2) + b + 1)
                    cols = slice(b * N, (b + 1) * N)
                    for a, zz in ((0, sum0), (1, sum1)):
                        mm = nc.tensor.matmul(pt[:, NB * (m % 2) + b, :], wA[:, a, m * P:(m + 1) * P],
                                              zz[:, cols], start=(a == 0), stop=(a == 1))
                    mm.then_inc(hA_mm, 1)
            pe.wait_ge(hA_ready, NB * M1)
            for m in range(M2):
                for b in range(NB):
                    dst = y0[:, b, :] if m == 0 else y1[:, b, :]
                    for a in range(M1):
                        mm = nc.tensor.matmul(dst, wB[:, a, m * P:(m + 1) * P], hA[a][:, b, :],
                                              start=(a == 0), stop=(a == M1 - 1))
                    mm.then_inc(hB_mm, 1)
            pe.wait_ge(hB_ready, NB * M2)
            for b in range(NB):
                for m in range(M2):
                    mm = nc.tensor.matmul(pt[0:1, b, :], wC[:, m:m + 1], hB[m][:, b, :],
                                          start=(m == 0), stop=(m == M2 - 1))
                mm.then_inc(y_mm, 1)


_TABLES = [f"tbl_{f}" for f in range(FIELDS)]
_INS = ["dense_ctx", "ids"] + _TABLES + ["W_top1", "b_top1", "W_top2", "b_top2", "W_top3",
                                         "L0_rec_w0", "L0_rec_b0", "L0_rec_w1", "L0_rec_b1"]


def kernel(**inputs):
    import concourse.bacc as bacc
    from concourse.bass_utils import run_bass_kernel_spmd

    nc = bacc.Bacc("TRN2", target_bir_lowering=False, num_devices=1)
    arrays, aps = {}, {}
    for name in _INS:
        a = np.ascontiguousarray(inputs[name])
        arrays[f"in_{name}"] = a
        aps[name] = nc.dram_tensor(f"in_{name}", a.shape, mybir.dt.from_np(a.dtype), kind="ExternalInput").ap()
    out = nc.dram_tensor("out_y", (inputs["ids"].shape[0], 1), F32, kind="ExternalOutput").ap()
    build(nc, aps["dense_ctx"], aps["ids"], [aps[t] for t in _TABLES], aps["W_top1"], aps["b_top1"],
          aps["W_top2"], aps["b_top2"], aps["W_top3"], aps["L0_rec_w0"], aps["L0_rec_b0"],
          aps["L0_rec_w1"], aps["L0_rec_b1"], out)
    r = run_bass_kernel_spmd(nc, [arrays], core_ids=[0])
    return r.results[0]["out_y"]
```

```python
from contextlib import ExitStack

import numpy as np

import concourse.bass as bass
from concourse import mybir

F32 = mybir.dt.float32
F32R = mybir.dt.float32r
I32 = mybir.dt.int32
ALU = mybir.AluOpType
ACT = mybir.ActivationFunctionType
AX_X = mybir.AxisListType.X

P = 128
FIELDS = 32
DIM = 64
HID = 64
OUT = 128
N = 512
SPT = N // DIM
ROT = 4
STEP = 4
HALF = 16
LEFT = 16
W2 = 2 * FIELDS
U = {(0, 0): 0, (0, 1): 31, (1, 0): 30, (1, 1): 31}
SPLIT1 = 3
TPB = 4


def build(nc, dense, ids, tables, W_top1, b_top1, W_top2, b_top2, W_top3, w0, b0, w1, b1, out):
    B = ids.shape[0]
    TILES = B // SPT
    BODIES = TILES // TPB
    GT = B // P
    DENSE = dense.shape[1]
    H1, H2 = W_top1.shape[1], W_top2.shape[1]
    M1, M2 = H1 // P, H2 // P
    assert FIELDS * 2 == HID == DIM and len(tables) == FIELDS and BODIES % GT == 0

    x_dram = nc.dram_tensor("x_rows", (2 * FIELDS, B * DIM), F32, kind="Internal").ap()
    ROW = B * DIM

    with ExitStack() as ctx:
        def sb(name, shape, dt=F32):
            return ctx.enter_context(nc.sbuf_tensor(name, shape, dt))

        def ps(name, shape):
            return ctx.enter_context(nc.psum_tensor(name, shape, F32))

        def sem(name):
            return ctx.enter_context(nc.semaphore(name))

        xrot = sb("xrot", [P, TPB, ROT, N])
        xoth = sb("xoth", [P, TPB, N])
        xlow = sb("xlow", [2 * LEFT, 2, N])
        xhigh = sb("xhigh", [2 * LEFT, 2, N])
        hid = sb("hid", [P, 2, ROT, N])
        z1 = sb("z1", [P, ROT - 1, ROT, N])
        zs = sb("zs", [P, ROT, N])
        zsh = sb("zsh", [P, SPLIT1, N], F32R)
        zsl = sb("zsl", [P, SPLIT1, N], F32R)
        z0 = sb("z0", [P, ROT, N])
        z0h = sb("z0h", [P, 2, ROT, N], F32R)
        z0l = sb("z0l", [P, ROT, N], F32R)
        zp = sb("zp", [2 * LEFT, N])
        zps = sb("zps", [P, N], F32R)
        sum0 = sb("sum0", [P, B])
        sum1 = sb("sum1", [P, B])
        rows = sb("rows", [P, FIELDS, DIM])
        idt = sb("idt", [P, FIELDS], I32)
        w0h = sb("w0h", [P, ROT, OUT], F32R)
        w0l = sb("w0l", [P, ROT, OUT], F32R)
        wp = sb("wp", [P, 2, OUT], F32R)
        w1T = sb("w1T", [P, ROT * ROT - SPLIT1, OUT])
        wsh = sb("wsh", [P, SPLIT1, OUT], F32R)
        wsl = sb("wsl", [P, SPLIT1, OUT], F32R)
        ident = sb("ident", [P, P])
        bias0 = sb("bias0", [P, 1])
        bias1 = sb("bias1", [P, 1])
        biasA = sb("biasA", [P, M1])
        biasB = sb("biasB", [P, M2])
        wA = sb("wA", [P, 2, H1])
        wB = sb("wB", [P, M1, H2])
        wC = sb("wC", [P, M2])
        dn = sb("dn", [P, B // P, DENSE])
        yrow = sb("yrow", [1, B])
        flat = z1[:, :, :, :].rearrange("p i a b -> p (i a b)")
        w1n = z0[:, :, :].rearrange("p a b -> p (a b)")
        w1d = flat[:, 0:(HID + ROT) * W2]
        walks = zs[:, :, :].rearrange("p i (j r) -> p i j r", j=ROT)
        w0n = hid[:, 0, 0:2, :].rearrange("p a b -> p (a b)")
        w0d = xrot[:, 0:2, :, :].rearrange("p t a b -> p (t a b)")
        fold = hid[:, 1, :, :].rearrange("p a b -> p (a b)")[:, 0:(ROT + 2) * P].rearrange(
            "p (k r) -> p k r", k=ROT + 2)
        hA = [flat[:, B * m:B * (m + 1)].rearrange("p (b n) -> p b n", n=N) for m in range(M1)]
        hB = [z0[:, (B // N) * m:(B // N) * (m + 1), :] for m in range(M2)]

        y0 = ps("y0", [P, 2, N])
        y1 = ps("y1", [P, 2, N])
        pt = ps("pt", [P, 4, N])

        weight_banks = [pt[:, 2, :], pt[:, 3, :], y0[:, 0, :], y0[:, 1, :], y1[:, 0, :], y1[:, 1, :]]

        ident_zero = sem("ident_zero")
        ident_ready = sem("ident_ready")
        ids_in = sem("ids_in")
        ids_seen = sem("ids_seen")
        gathered = sem("gathered")
        x_written = sem("x_written")
        w_in = sem("w_in")
        top_in = sem("top_in")
        zeroed = sem("zeroed")
        w0_repeated = sem("w0_repeated")
        w1_repeated = sem("w1_repeated")
        w1_walked = sem("w1_walked")
        w0_folded = sem("w0_folded")
        w_turned = sem("w_turned")
        w_high = sem("w_high")
        w_low = sem("w_low")
        dense_turned = sem("dense_turned")
        dense_ready = sem("dense_ready")
        x_in = [sem(f"x_in{s}") for s in range(TPB)]
        hid_in = [[None] + [sem(f"hid_in{s}_{i}") for i in range(1, ROT)] for s in range(2)]
        z0_made = sem("z0_made")
        z0_high = sem("z0_high")
        z0_low = sem("z0_low")
        zp_made = sem("zp_made")
        zp_high = sem("zp_high")
        zp_low = sem("zp_low")
        zp_ready = sem("zp_ready")
        zs_made = sem("zs_made")
        zs_high = sem("zs_high")
        zs_low = sem("zs_low")
        l0_done = sem("l0_done")
        hid_ready = sem("hid_ready")
        direct_summed = sem("direct_summed")
        z1_ready = sem("z1_ready")
        l1_blocks = sem("l1_blocks")
        last_summed = sem("last_summed")
        hA_mm = sem("hA_mm")
        hA_ready = sem("hA_ready")
        hB_mm = sem("hB_mm")
        hB_ready = sem("hB_ready")
        y_mm = sem("y_mm")
        y_ready = sem("y_ready")
        y_out = sem("y_out")

        X_LOADS = [8, 6, 8, 6]
        block = ctx.enter_context(nc.Block())

        def at_least(eng, s, value):
            if not isinstance(value, int) or value > 0:
                eng.wait_ge(s, value)

        def view(ap, offset, dims):
            return bass.AP(ap.tensor, ap.offset + offset, [list(ap.ap[0])] + [list(d) for d in dims])

        @block.gpsimd
        def _(pool):
            nc.gpsimd.memset(ident[:], 0.0).then_inc(ident_zero, 1)
            pool.wait_ge(ident_zero, 1)
            nc.gpsimd.affine_select(out=ident[:], in_=ident[:], compare_op=ALU.not_equal, fill=1.0, base=0,
                                    pattern=[[-1, P]], channel_multiplier=1).then_inc(ident_ready, 1)

            def gather(g, first):
                if not first:
                    pool.wait_ge(x_written, g * 32)
                pool.dma_start(idt[:], ids[bass.ds(g * P, P), :]).then_inc(ids_in, 16)
                pool.wait_ge(ids_in, (g + 1) * 16)
                pool.sem_inc(ids_seen, 1)
                for f in range(FIELDS):
                    pool.indirect_dma_start(
                        out=rows[:, f, :], out_offset=None, in_=tables[f],
                        in_offset=bass.IndirectOffsetOnAxis(ap=idt[:, f:f + 1], axis=0),
                    ).then_inc(gathered, 16)
                pool.wait_ge(gathered, (g + 1) * (16 * FIELDS))
                for copy in range(2):
                    dst = bass.AP(x_dram.tensor, x_dram.offset + copy * FIELDS * ROW + g * (P * DIM),
                                  [[DIM, P], [ROW, FIELDS], [1, DIM]])
                    pool.dma_start(dst, rows[:]).then_inc(x_written, 16)

            gather(0, True)
            with pool.Fori(1, GT) as g:
                gather(g, False)
            pool.wait_ge(x_written, GT * 32)

        @block.sync
        def _(sp):
            sp.dma_start(w0n, w0).then_inc(w_in, 16)
            sp.dma_start(w1n, w1).then_inc(w_in, 16)
            sp.dma_start(bias0[:], b0.rearrange("(p a) -> p a", a=1)).then_inc(w_in, 16)
            sp.dma_start(bias1[:], b1.rearrange("(p a) -> p a", a=1)).then_inc(w_in, 16)

            def load_x(t, s):
                base = x_dram.offset + t * N
                for c in range(2):
                    for h in range(2):
                        g = 64 * c + 32 * h
                        src = bass.AP(x_dram.tensor, base + HALF * c * ROW,
                                      [[ROW, FIELDS], [STEP * ROW, ROT], [1, N]])
                        sp.dma_start(xrot[g:g + 32, s, :, :], src).then_inc(x_in[s], 16)
                for c in range(2):
                    d = U[c, 1] - U[c, 0]
                    src = bass.AP(x_dram.tensor, base + U[c, 0] * ROW,
                                  [[d * ROW, 2], [ROW, FIELDS], [1, N]])
                    sp.dma_start(xoth[64 * c:64 * c + 64, s, :], src).then_inc(x_in[s], 16)
                if s % 2 == 0:
                    for dst, field in ((xlow, 0), (xhigh, HALF)):
                        src = bass.AP(x_dram.tensor, base + field * ROW, [[ROW, LEFT], [N, 2], [1, N]])
                        sp.dma_start(dst[:, s // 2, :], src).then_inc(x_in[s], 16)

            def rotate_hidden(t, s):
                sp.wait_ge(hid_ready, 2 * t + 2)
                for i in range(1, ROT):
                    for c in range(2):
                        sp.dma_start(hid[HID * c:HID * (c + 1), s, i, :],
                                     hid[i:i + HID, s, 0, :]).then_inc(hid_in[s][i], 16)

            sp.dma_start(dn[:], dense.rearrange("(q p) c -> p q c", p=P)).then_inc(top_in, 16)
            sp.dma_start(wA[64:128, 0, :], W_top1[0:HID, :]).then_inc(top_in, 16)
            sp.wait_ge(zeroed, 3)
            sp.dma_start(wA[0:DENSE, 0, :], W_top1[HID + OUT:HID + OUT + DENSE, :]).then_inc(top_in, 16)
            sp.dma_start(wA[:, 1, :], W_top1[HID:HID + OUT, :]).then_inc(top_in, 16)
            sp.dma_start(wB[:], W_top2.rearrange("(m p) n -> p m n", p=P)).then_inc(top_in, 16)
            with nc.allow_non_contiguous_dma(reason="a few hundred bias and weight values"):
                sp.dma_start(wC[:], W_top3.rearrange("(m p) a -> p (m a)", p=P)).then_inc(top_in, 16)
                sp.dma_start(biasA[:], b_top1.rearrange("(m p) -> p m", p=P)).then_inc(top_in, 16)
                sp.dma_start(biasB[:], b_top2.rearrange("(m p) -> p m", p=P)).then_inc(top_in, 16)
            sp.wait_ge(x_written, 32)
            sp.wait_ge(w0_folded, 9)
            for t in range(TPB):
                load_x(t, t)
            rotate_hidden(0, 0)

            def body(k, more):
                for q in range(TPB):
                    t = k * TPB + q
                    if more or q < TPB - 1:
                        rotate_hidden(t + 1, (q + 1) % 2)
                    if more:
                        sp.wait_ge(z1_ready, (t + 1) * (ROT - 1))
                        load_x(t + TPB, q)

            BPG = BODIES // GT
            for k in range(BPG - 1):
                body(k, True)
            with sp.Fori(1, GT) as g:
                sp.wait_ge(x_written, g * 32 + 32)
                for j in range(BPG):
                    body(g * BPG + (j - 1), True)
            body(BODIES - 1, False)
            sp.wait_ge(y_ready, B // N)
            sp.dma_start(out.rearrange("b a -> a b"), yrow[0:1, :]).then_inc(y_out, 16)
            sp.wait_ge(y_out, 16)

        @block.scalar
        def _(act):
            for i in range(ROT):
                act.wait_ge(w_turned, i + 1)
                bank = weight_banks[i + 2].rearrange("p (a b) -> p a b", a=ROT)
                if i == 0:
                    nc.scalar.activation(wsh[:], bank[:, 0:SPLIT1, :], ACT.Copy).then_inc(w_high, 1)
                    nc.scalar.activation(w1T[:, 0:ROT - SPLIT1, :], bank[:, SPLIT1:, :], ACT.Copy).then_inc(w_high, 1)
                else:
                    nc.scalar.activation(w1T[:, ROT * i - SPLIT1:ROT * (i + 1) - SPLIT1, :], bank,
                                         ACT.Copy).then_inc(w_high, 1)
            act.wait_ge(w_turned, ROT + 1)
            nc.scalar.activation(w0h[:], weight_banks[0].rearrange("p (a b) -> p a b", a=ROT),
                                 ACT.Copy).then_inc(w_high, 1)
            act.wait_ge(w_turned, ROT + 2)
            nc.scalar.activation(wp[:], weight_banks[1][:, 0:2 * OUT].rearrange("p (a b) -> p a b", a=2),
                                 ACT.Copy).then_inc(w_high, 1)
            act.wait_ge(w_in, 64)
            act.wait_ge(zeroed, 3)
            act.wait_ge(dense_turned, 1)
            nc.scalar.activation(sum0[0:DENSE, :], pt[0:DENSE, 0:B // N, :].rearrange("p a b -> p (a b)"),
                                 ACT.Copy).then_inc(dense_ready, 1)

            def hidden_out(t, s):
                act.wait_ge(l0_done, t + 1)
                at_least(act, z1_ready, (t - 1) * (ROT - 1))
                for c in range(2):
                    nc.scalar.activation(hid[64 * c:64 * c + 64, s, 0, :], y0[0:HID, s, :], ACT.Relu,
                                         bias=bias0[0:HID, :]).then_inc(hid_ready, 1)

            def direct_out(t, s):
                for a in range(SPT):
                    part = y0[HID:OUT, s, a * DIM:(a + 1) * DIM]
                    nc.scalar.activation(part, part, ACT.Relu, bias=bias0[HID:OUT, :],
                                         accum_out=sum0[HID:OUT, bass.ds(t * SPT + a, 1)]).then_inc(direct_summed, 1)

            def layer1_out(t, s):
                act.wait_ge(l1_blocks, (t + 1) * ROT)
                for a in range(SPT):
                    part = y1[:, s, a * DIM:(a + 1) * DIM]
                    nc.scalar.activation(part, part, ACT.Relu, bias=bias1[:],
                                         accum_out=sum1[:, bass.ds(t * SPT + a, 1)]).then_inc(last_summed, 1)

            def round0(t, s):
                act.wait_ge(z0_made, t + 1)
                at_least(act, l0_done, t - 1)
                nc.scalar.activation(z0h[:, s, :, :], z0[:], ACT.Copy).then_inc(z0_high, 1)

            def round_pair(pair):
                act.wait_ge(zp_made, pair + 1)
                at_least(act, l0_done, 2 * pair)
                for r in (0, 32):
                    nc.scalar.activation(zps[r:r + 32, :], zp[:], ACT.Copy).then_inc(zp_high, 1)

            def repeat_low(pair):
                act.wait_ge(zp_low, pair + 1)
                nc.scalar.activation(zps[96:128, :], zps[64:96, :].bitcast(F32), ACT.Copy).then_inc(zp_ready, 1)

            def round_split(t):
                act.wait_ge(zs_made, t + 1)
                at_least(act, l1_blocks, (t - 1) * ROT + 1)
                nc.scalar.activation(zsh[:], zs[:, 0:SPLIT1, :], ACT.Copy).then_inc(zs_high, 1)

            def body(k, first, more):
                for q in range(TPB):
                    t = k * TPB + q
                    pair = k * 2 + (q // 2 + 1)
                    if more or q < TPB - 1:
                        hidden_out(t + 1, (q + 1) % 2)
                    if q % 2 == 0 and (more or q < 2):
                        round_pair(pair)
                    if more or q < TPB - 1:
                        direct_out(t + 1, (q + 1) % 2)
                    if not (first and q == 0):
                        layer1_out(t - 1, (q + 1) % 2)
                    if q % 2 == 0 and (more or q < 2):
                        repeat_low(pair)
                    if more or q < TPB - 1:
                        round_split(t + 1)
                    if more or q < 1:
                        round0(t + 3, (q + 1) % 2)

            round0(0, 0)
            round_pair(0)
            repeat_low(0)
            round0(1, 1)
            hidden_out(0, 0)
            direct_out(0, 0)
            round_split(0)
            round0(2, 0)
            body(0, True, True)
            with act.Fori(1, BODIES - 1) as k:
                body(k, False, True)
            body(BODIES - 1, False, False)
            layer1_out(TILES - 1, (TILES - 1) % 2)

            act.wait_ge(top_in, 8 * 16)
            for m in range(M1):
                for b in range(B // N):
                    act.wait_ge(hA_mm, (B // N) * m + b + 1)
                    nc.scalar.activation(hA[m][:, b, :], pt[:, (B // N) * (m % 2) + b, :], ACT.Relu,
                                         bias=biasA[:, m:m + 1]).then_inc(hA_ready, 1)
            for m in range(M2):
                for b in range(B // N):
                    act.wait_ge(hB_mm, (B // N) * m + b + 1)
                    nc.scalar.activation(hB[m][:, b, :], y0[:, b, :] if m == 0 else y1[:, b, :], ACT.Relu,
                                         bias=biasB[:, m:m + 1]).then_inc(hB_ready, 1)
            for b in range(B // N):
                act.wait_ge(y_mm, b + 1)
                nc.scalar.activation(yrow[0:1, b * N:(b + 1) * N], pt[0:1, b, :], ACT.Copy).then_inc(y_ready, 1)

        @block.vector
        def _(dve):
            nc.vector.memset(sum0[:], 0.0).then_inc(zeroed, 1)
            nc.vector.memset(wA[0:64, 0, :], 0.0).then_inc(zeroed, 1)
            nc.vector.memset(fold[:, ROT:, :], 0.0).then_inc(zeroed, 1)
            dve.wait_ge(w_in, 64)
            w0v = w0n.rearrange("p (h f) -> p h f", h=FIELDS)
            w0dv = w0d.rearrange("p (h f) -> p h f", h=W2)
            for a in range(2):
                for b in range(2):
                    nc.vector.tensor_copy(w0dv[:, FIELDS * a:FIELDS * (a + 1), FIELDS * b:FIELDS * (b + 1)],
                                          w0v).then_inc(w0_repeated, 1)
            w1v = w1n.rearrange("p (h f) -> p h f", h=HID)
            w1dv = w1d.rearrange("p (h f) -> p h f", f=W2)
            for b in range(2):
                nc.vector.tensor_copy(w1dv[:, 0:HID, FIELDS * b:FIELDS * (b + 1)], w1v).then_inc(w1_repeated, 1)
                nc.vector.tensor_copy(w1dv[:, HID:HID + ROT, FIELDS * b:FIELDS * (b + 1)],
                                      w1v[:, 0:ROT, :]).then_inc(w1_repeated, 1)
            dve.wait_ge(w1_repeated, 4)
            for i in range(ROT):
                for c in range(2):
                    nc.vector.tensor_copy(
                        walks[:, i, :, 64 * c:64 * c + 64].rearrange("p j (h q) -> p j h q", h=2),
                        view(w1d, i * W2 + HALF * c,
                             [[STEP, ROT], [FIELDS * W2, 2], [W2 + 1, FIELDS]])).then_inc(w1_walked, 1)
            dve.wait_ge(w0_repeated, 4)
            dve.wait_ge(zeroed, 3)
            for c in range(2):
                for h in range(2):
                    u = U[c, h]
                    nc.vector.tensor_tensor(
                        fold[:, 0:ROT, 64 * c + 32 * h:64 * c + 32 * h + 32],
                        view(w0d, HALF * c * W2 + u, [[STEP * W2, ROT], [W2 + 1, FIELDS]]),
                        view(w0d, u * W2 + HALF * c, [[STEP, ROT], [W2 + 1, FIELDS]]),
                        ALU.add).then_inc(w0_folded, 1)
            for b in range(2):
                for both in range(2):
                    dst = fold[:, ROT + b, :].rearrange("p (c r b) -> p c r b", b=2, r=LEFT)[:, :, :, b]
                    src = view(w0d, HALF * (W2 if both else 1), [[0, 4], [W2 + 1, LEFT]])
                    if both:
                        dve.wait_ge(w0_folded, 5 + 2 * b)
                        nc.vector.tensor_tensor(dst, dst, src, ALU.add).then_inc(w0_folded, 1)
                    else:
                        nc.vector.tensor_copy(dst, src).then_inc(w0_folded, 1)
            dve.wait_ge(w0_folded, 8)
            nc.vector.tensor_copy(fold[:, 0, 0:FIELDS], view(w0d, 0, [[W2 + 1, FIELDS]])).then_inc(w0_folded, 1)

            dve.wait_ge(w_high, ROT + 3)
            bank = weight_banks[2].rearrange("p (a b) -> p a b", a=ROT)
            nc.vector.tensor_tensor(wsl[:], bank[:, 0:SPLIT1, :], wsh[:].bitcast(F32),
                                    ALU.subtract).then_inc(w_low, 1)
            nc.vector.tensor_tensor(w0l[:], weight_banks[0].rearrange("p (a b) -> p a b", a=ROT),
                                    w0h[:].bitcast(F32), ALU.subtract).then_inc(w_low, 1)
            for r in (32, 96):
                nc.vector.tensor_tensor(wp[r:r + 32, :, :],
                                        weight_banks[1][r:r + 32, 0:2 * OUT].rearrange("p (a b) -> p a b", a=2),
                                        wp[r:r + 32, :, :].bitcast(F32), ALU.subtract).then_inc(w_low, 1)

            def products0(t, s):
                dve.wait_ge(x_in[s], (t - s) * (4 * X_LOADS[s]) + 16 * X_LOADS[s])
                at_least(dve, z0_low, t)
                nc.vector.tensor_tensor(z0[:], xoth[:, s:s + 1, :].to_broadcast([P, ROT, N]),
                                        xrot[:, s, :, :], ALU.mult).then_inc(z0_made, 1)

            def products_pair(pair, s):
                at_least(dve, zp_low, pair)
                nc.vector.tensor_tensor(zp[:], xlow[:, s, :], xhigh[:, s, :], ALU.mult).then_inc(zp_made, 1)

            def low0(t, s):
                dve.wait_ge(z0_high, t + 1)
                at_least(dve, l0_done, t)
                nc.vector.tensor_tensor(z0l[:], z0[:], z0h[:, s, :, :].bitcast(F32),
                                        ALU.subtract).then_inc(z0_low, 1)

            def low_pair(pair):
                dve.wait_ge(zp_high, pair * 2 + 2)
                nc.vector.tensor_tensor(zps[64:96, :], zp[:], zps[0:32, :].bitcast(F32),
                                        ALU.subtract).then_inc(zp_low, 1)

            def products1(i, t, s, xs):
                if i == 0:
                    dve.wait_ge(hid_ready, 2 * t + 2)
                    at_least(dve, zs_low, t)
                else:
                    dve.wait_ge(hid_in[s][i], (t - s) * 16 + 32)
                at_least(dve, l1_blocks, (t - 1) * ROT + (i + 1))
                nc.vector.tensor_tensor(zs[:] if i == 0 else z1[:, i - 1, :, :],
                                        hid[:, s, i:i + 1, :].to_broadcast([P, ROT, N]),
                                        xrot[:, xs, :, :], ALU.mult).then_inc(zs_made if i == 0 else z1_ready, 1)

            def low_split(t):
                dve.wait_ge(zs_high, t + 1)
                at_least(dve, l1_blocks, (t - 1) * ROT + 1)
                nc.vector.tensor_tensor(zsl[:], zs[:, 0:SPLIT1, :], zsh[:].bitcast(F32),
                                        ALU.subtract).then_inc(zs_low, 1)

            def body(k, more):
                for q in range(TPB):
                    t = k * TPB + q
                    at = (t, q % 2, q)
                    ahead = more or q < 2
                    pair = k * 2 + (q // 2 + 1)
                    products1(0, *at)
                    products1(1, *at)
                    low_split(t)
                    if ahead:
                        products0(t + 2, (q + 2) % TPB)
                        if q % 2 == 0:
                            products_pair(pair, (q // 2 + 1) % 2)
                    products1(2, *at)
                    products1(3, *at)
                    if ahead:
                        low0(t + 2, q % 2)
                        if q % 2 == 0:
                            low_pair(pair)

            products0(0, 0)
            products_pair(0, 0)
            low0(0, 0)
            low_pair(0)
            products0(1, 1)
            low0(1, 1)
            dve.wait_ge(w_turned, ROT + 2)
            body(0, True)
            with dve.Fori(1, BODIES - 1) as k:
                body(k, True)
            body(BODIES - 1, False)

        @block.tensor
        def _(pe):
            pe.wait_ge(ident_ready, 1)
            pe.wait_ge(w1_walked, 2 * ROT)
            for i in range(ROT):
                for j in range(ROT):
                    turned = nc.tensor.transpose(weight_banks[i + 2][:, j * OUT:(j + 1) * OUT],
                                                 walks[:, i, j, :], ident[:])
                turned.then_inc(w_turned, 1)
            pe.wait_ge(w0_folded, 9)
            for j in range(ROT):
                turned = nc.tensor.transpose(weight_banks[0][:, j * OUT:(j + 1) * OUT], fold[:, j, :], ident[:])
            turned.then_inc(w_turned, 1)
            for b in range(2):
                turned = nc.tensor.transpose(weight_banks[1][:, b * OUT:(b + 1) * OUT], fold[:, ROT + b, :], ident[:])
            turned.then_inc(w_turned, 1)
            pe.wait_ge(top_in, 8 * 16)
            for q in range(B // P):
                turned = nc.tensor.transpose(pt[0:DENSE, q // 4, (q % 4) * P:(q % 4 + 1) * P], dn[:, q, :], ident[:])
            turned.then_inc(dense_turned, 1)
            pe.wait_ge(w_low, 4)

            def layer0(t, s):
                pe.wait_ge(z0_low, t + 1)
                pe.wait_ge(zp_ready, (t - s) // 2 + 1)
                at_least(pe, direct_summed, (t - 1) * SPT)
                nc.tensor.matmul(y0[:, s, :], wp[:, s, :], zps[:], start=True, stop=False)
                for j in range(ROT):
                    for w, z in ((w0h, z0h), (w0l, z0h), (w0h, z0l)):
                        mm = nc.tensor.matmul(y0[:, s, :], w[:, j, :],
                                              z0l[:, j, :] if z is z0l else z0h[:, s, j, :], start=False,
                                              stop=(j == ROT - 1 and z is z0l))
                mm.then_inc(l0_done, 1)

            def layer1(t, s):
                at_least(pe, last_summed, (t - 1) * SPT)
                for i in range(ROT):
                    if i == 0:
                        pe.wait_ge(zs_low, t + 1)
                        for j in range(SPLIT1):
                            for w, z in ((wsh, zsh), (wsl, zsh), (wsh, zsl)):
                                mm = nc.tensor.matmul(y1[:, s, :], w[:, j, :], z[:, j, :],
                                                      start=(j == 0 and w is wsh and z is zsh), stop=False)
                    else:
                        pe.wait_ge(z1_ready, t * (ROT - 1) + i)
                    for j in range(SPLIT1 if i == 0 else 0, ROT):
                        mm = nc.tensor.matmul(y1[:, s, :], w1T[:, ROT * i + j - SPLIT1, :],
                                              zs[:, j, :] if i == 0 else z1[:, i - 1, j, :],
                                              start=False, stop=(i == ROT - 1 and j == ROT - 1))
                    mm.then_inc(l1_blocks, 1)

            def body(k, more):
                for q in range(TPB):
                    t = k * TPB + q
                    if more or q < TPB - 1:
                        layer0(t + 1, (q + 1) % 2)
                    layer1(t, q % 2)

            layer0(0, 0)
            body(0, True)
            with pe.Fori(1, BODIES - 1) as k:
                body(k, True)
            body(BODIES - 1, False)

            pe.wait_ge(dense_ready, 1)
            pe.wait_ge(direct_summed, B)
            pe.wait_ge(last_summed, B)
            NB = B // N
            for m in range(M1):
                for b in range(NB):
                    if m >= 2:
                        pe.wait_ge(hA_ready, NB * (m - 2) + b + 1)
                    cols = slice(b * N, (b + 1) * N)
                    for a, zz in ((0, sum0), (1, sum1)):
                        mm = nc.tensor.matmul(pt[:, NB * (m % 2) + b, :], wA[:, a, m * P:(m + 1) * P],
                                              zz[:, cols], start=(a == 0), stop=(a == 1))
                    mm.then_inc(hA_mm, 1)
            pe.wait_ge(hA_ready, NB * M1)
            for m in range(M2):
                for b in range(NB):
                    dst = y0[:, b, :] if m == 0 else y1[:, b, :]
                    for a in range(M1):
                        mm = nc.tensor.matmul(dst, wB[:, a, m * P:(m + 1) * P], hA[a][:, b, :],
                                              start=(a == 0), stop=(a == M1 - 1))
                    mm.then_inc(hB_mm, 1)
            pe.wait_ge(hB_ready, NB * M2)
            for b in range(NB):
                for m in range(M2):
                    mm = nc.tensor.matmul(pt[0:1, b, :], wC[:, m:m + 1], hB[m][:, b, :],
                                          start=(m == 0), stop=(m == M2 - 1))
                mm.then_inc(y_mm, 1)


_TABLES = [f"tbl_{f}" for f in range(FIELDS)]
_INS = ["dense_ctx", "ids"] + _TABLES + ["W_top1", "b_top1", "W_top2", "b_top2", "W_top3",
                                         "L0_rec_w0", "L0_rec_b0", "L0_rec_w1", "L0_rec_b1"]


def kernel(**inputs):
    import concourse.bacc as bacc
    from concourse.bass_utils import run_bass_kernel_spmd

    nc = bacc.Bacc("TRN2", target_bir_lowering=False, num_devices=1)
    arrays, aps = {}, {}
    for name in _INS:
        a = np.ascontiguousarray(inputs[name])
        arrays[f"in_{name}"] = a
        aps[name] = nc.dram_tensor(f"in_{name}", a.shape, mybir.dt.from_np(a.dtype), kind="ExternalInput").ap()
    out = nc.dram_tensor("out_y", (inputs["ids"].shape[0], 1), F32, kind="ExternalOutput").ap()
    build(nc, aps["dense_ctx"], aps["ids"], [aps[t] for t in _TABLES], aps["W_top1"], aps["b_top1"],
          aps["W_top2"], aps["b_top2"], aps["W_top3"], aps["L0_rec_w0"], aps["L0_rec_b0"],
          aps["L0_rec_w1"], aps["L0_rec_b1"], out)
    r = run_bass_kernel_spmd(nc, [arrays], core_ids=[0])
    return r.results[0]["out_y"]
```

```python
from contextlib import ExitStack

import numpy as np

import concourse.bass as bass
from concourse import mybir

F32 = mybir.dt.float32
F32R = mybir.dt.float32r
I32 = mybir.dt.int32
ALU = mybir.AluOpType
ACT = mybir.ActivationFunctionType

P = 128
FIELDS = 32
DIM = 64
HID = 64
OUT = 128
N = 512
SPT = N // DIM
ROT = 4
STEP = 4
HALF = 16
GROUP = 8
LEFT = 16
W2 = 2 * FIELDS
U = {(0, 0): 0, (0, 1): 31, (1, 0): 30, (1, 1): 31}
ORDER1 = (1, 0, 2, 3)
TPB = 4


def build(nc, dense, ids, tables, W_top1, b_top1, W_top2, b_top2, W_top3, w0, b0, w1, b1, out):
    B = ids.shape[0]
    TILES = B // SPT
    BODIES = TILES // TPB
    GT = B // P
    DENSE = dense.shape[1]
    H1, H2 = W_top1.shape[1], W_top2.shape[1]
    M1, M2 = H1 // P, H2 // P
    assert M1 == ROT and B == 2 * N
    assert FIELDS * 2 == HID == DIM and len(tables) == FIELDS and BODIES % GT == 0
    assert 8 * LEFT == P and TPB == 4

    x_dram = nc.dram_tensor("x_rows", (2 * FIELDS, B * DIM), F32, kind="Internal").ap()
    ROW = B * DIM

    with ExitStack() as ctx:
        def sb(name, shape, dt=F32):
            return ctx.enter_context(nc.sbuf_tensor(name, shape, dt))

        def ps(name, shape):
            return ctx.enter_context(nc.psum_tensor(name, shape, F32))

        def sem(name):
            return ctx.enter_context(nc.semaphore(name))

        xrot = sb("xrot", [P, TPB, ROT, N])
        xoth = sb("xoth", [P, TPB, N])
        xlow = sb("xlow", [P, N])
        xhigh = sb("xhigh", [P, N])
        hid = sb("hid", [P, 2, ROT, N])
        z1 = sb("z1", [P, ROT - 1, ROT, N])
        zs = sb("zs", [P, ROT, N])
        zsh = sb("zsh", [P, ROT, N], F32R)
        zsl = sb("zsl", [P, ROT, N], F32R)
        z0 = sb("z0", [P, ROT, N])
        z0h = sb("z0h", [P, 2, ROT, N], F32R)
        z0l = sb("z0l", [P, ROT, N], F32R)
        zq = sb("zq", [P, N])
        zql = sb("zql", [P, N], F32R)
        zps = sb("zps", [P, N], F32R)
        sums = sb("sums", [P, 2, B])
        sum0 = sums[:, 0, :]
        sum1 = sums[:, 1, :]
        rows = sb("rows", [P, FIELDS, DIM])
        all_ids = sb("all_ids", [P, B // P, FIELDS], I32)
        idt = sb("idt", [P, FIELDS], I32)
        w0h = sb("w0h", [P, ROT, OUT], F32R)
        w0l = sb("w0l", [P, ROT, OUT], F32R)
        wp = sb("wp", [P, 2, OUT], F32R)
        w1T = sb("w1T", [P, ROT - 1, ROT, OUT])
        wsh = sb("wsh", [P, ROT, OUT], F32R)
        wsl = sb("wsl", [P, ROT, OUT], F32R)
        ident = sb("ident", [P, P])
        bias0 = sb("bias0", [P, 1])
        bias1 = sb("bias1", [P, 1])
        biasA = sb("biasA", [P, M1])
        biasB = sb("biasB", [P, M2])
        wAh = sb("wAh", [P, 2, H1], F32R)
        wAl = sb("wAl", [P, 2, H1], F32R)
        wBh = sb("wBh", [P, M1, H2], F32R)
        wBl = sb("wBl", [P, M1, H2], F32R)
        sum_parts = sb("sum_parts", [P, 2, 2, N], F32R)
        wC = sb("wC", [P, M2])
        dn = sb("dn", [P, B // P, DENSE])
        yrow = sb("yrow", [1, B])
        flat = z1[:, :, :, :].rearrange("p i a b -> p (i a b)")
        w1n = z0[:, :, :].rearrange("p a b -> p (a b)")
        w1d = flat[:, 0:(HID + ROT) * W2]
        walks = zs[:, :, :].rearrange("p i (j r) -> p i j r", j=ROT)
        w0n = hid[:, 0, 0:2, :].rearrange("p a b -> p (a b)")
        w0d = xrot[:, 0:2, :, :].rearrange("p t a b -> p (t a b)")
        fold = hid[:, 1, :, :].rearrange("p a b -> p (a b)")[:, 0:(ROT + 2) * P].rearrange(
            "p (k r) -> p k r", k=ROT + 2)
        late = xrot[:, 2, :, :].rearrange("p a b -> p (a b)")
        wA = late[:, 0:2 * H1].rearrange("p (a n) -> p a n", a=2)
        wB = late[:, 2 * H1:2 * H1 + M1 * H2].rearrange("p (m n) -> p m n", m=M1)
        hA = [flat[:, B * m:B * (m + 1)].rearrange("p (b n) -> p b n", n=N) for m in range(M1)]
        hAh = [[z0h[:, b, m, :] for m in range(M1)] for b in range(2)]
        hAl = [[z[:, m, :] for m in range(M1)] for z in (zsh, zsl)]
        sum_halves = [sum_parts[:, :, :, :], z0l[:, :, :].rearrange("p (a c) n -> p a c n", a=2)]
        hB = [z0[:, (B // N) * m:(B // N) * (m + 1), :] for m in range(M2)]

        y0 = ps("y0", [P, 2, N])
        y1 = ps("y1", [P, 2, N])
        pt = ps("pt", [P, 4, N])

        weight_banks = [pt[:, 2, :], pt[:, 3, :], y0[:, 0, :], y0[:, 1, :], y1[:, 0, :], y1[:, 1, :]]

        ident_zero = sem("ident_zero")
        ident_ready = sem("ident_ready")
        ids_in = sem("ids_in")
        ids_placed = sem("ids_placed")
        ids_seen = sem("ids_seen")
        gathered = [sem(f"gathered{n}") for n in range(FIELDS // GROUP)]
        x_first = sem("x_first")
        x_written = sem("x_written")
        w_in = sem("w_in")
        top_in = sem("top_in")
        zeroed = sem("zeroed")
        w0_repeated = sem("w0_repeated")
        w1_repeated = sem("w1_repeated")
        w1_walked = sem("w1_walked")
        w0_folded = sem("w0_folded")
        w_turned = sem("w_turned")
        w_high = sem("w_high")
        w_low = sem("w_low")
        top_high = sem("top_high")
        top_low = sem("top_low")
        sum_high = sem("sum_high")
        sum_low = sem("sum_low")
        hA_high = sem("hA_high")
        hA_low = sem("hA_low")
        dense_turned = sem("dense_turned")
        dense_ready = sem("dense_ready")
        x_in = [sem(f"x_in{s}") for s in range(TPB)]
        quad_in = sem("quad_in")
        hid_in = [[None] + [sem(f"hid_in{s}_{i}") for i in range(1, ROT)] for s in range(2)]
        z0_made = sem("z0_made")
        z0_high = sem("z0_high")
        z0_low = sem("z0_low")
        half_made = sem("half_made")
        half_high = sem("half_high")
        half_low = sem("half_low")
        quad_made = sem("quad_made")
        quad_high = sem("quad_high")
        quad_low = sem("quad_low")
        pair_ready = sem("pair_ready")
        zs_made = sem("zs_made")
        zs_high = sem("zs_high")
        zs_low = sem("zs_low")
        l0_done = sem("l0_done")
        hid_ready = sem("hid_ready")
        direct_summed = sem("direct_summed")
        z1_ready = sem("z1_ready")
        l1_blocks = sem("l1_blocks")
        last_summed = sem("last_summed")
        hA_mm = sem("hA_mm")
        hA_ready = sem("hA_ready")
        hB_mm = sem("hB_mm")
        hB_ready = sem("hB_ready")
        y_mm = sem("y_mm")
        y_ready = sem("y_ready")
        y_out = sem("y_out")

        X_LOADS = 6
        QUAD_LOADS = 4
        FIRST = TPB * SPT
        X_FIRST = 16 * (2 * len(gathered) + 2)
        block = ctx.enter_context(nc.Block())

        def at_least(eng, s, value):
            if not isinstance(value, int) or value > 0:
                eng.wait_ge(s, value)

        def view(ap, offset, dims):
            return bass.AP(ap.tensor, ap.offset + offset, [list(ap.ap[0])] + [list(d) for d in dims])

        @block.gpsimd
        def _(pool):
            nc.gpsimd.memset(ident[:], 0.0).then_inc(ident_zero, 1)
            pool.wait_ge(ident_zero, 1)
            nc.gpsimd.affine_select(out=ident[:], in_=ident[:], compare_op=ALU.not_equal, fill=1.0, base=0,
                                    pattern=[[-1, P]], channel_multiplier=1).then_inc(ident_ready, 1)

            pool.wait_ge(ids_in, 16)

            def gather(g, first):
                nc.gpsimd.tensor_copy(idt[:], all_ids[:, bass.ds(g, 1), :].rearrange("p a f -> p (a f)")
                                      ).then_inc(ids_placed, 1)
                pool.wait_ge(ids_placed, g + 1)
                pool.sem_inc(ids_seen, 1)
                for n, done in enumerate(gathered):
                    for f in range(n * GROUP, (n + 1) * GROUP):
                        pool.indirect_dma_start(
                            out=rows[:, f, :], out_offset=None, in_=tables[f],
                            in_offset=bass.IndirectOffsetOnAxis(ap=idt[:, f:f + 1], axis=0),
                        ).then_inc(done, 16)
                    if n and not first:
                        write_x(g, n - 1)
                if not first:
                    write_x(g, len(gathered) - 1)

            def write_x(g, n):
                pool.wait_ge(gathered[n], (g + 1) * (16 * GROUP))
                for copy in range(2):
                    dst = bass.AP(x_dram.tensor,
                                  x_dram.offset + (copy * FIELDS + n * GROUP) * ROW + g * (P * DIM),
                                  [[DIM, P], [ROW, GROUP], [1, DIM]])
                    pool.dma_start(dst, rows[:, n * GROUP:(n + 1) * GROUP, :]).then_inc(x_written, 16)

            gather(0, True)
            pool.wait_ge(x_first, X_FIRST)
            gather(1, False)
            with pool.Fori(2, GT) as g:
                pool.wait_ge(x_written, (g - 1) * (32 * len(gathered)))
                gather(g, False)
            pool.wait_ge(x_written, (GT - 1) * 32 * len(gathered))

        @block.sync
        def _(sp):
            sp.dma_start(all_ids[:], ids.rearrange("(q p) f -> p q f", p=P)).then_inc(ids_in, 16)
            sp.dma_start(w0n, w0).then_inc(w_in, 16)
            sp.dma_start(w1n, w1).then_inc(w_in, 16)
            sp.dma_start(bias0[:], b0.rearrange("(p a) -> p a", a=1)).then_inc(w_in, 16)
            sp.dma_start(bias1[:], b1.rearrange("(p a) -> p a", a=1)).then_inc(w_in, 16)

            def load_x(t, s):
                base = x_dram.offset + t * N
                for c in range(2):
                    for h in range(2):
                        g = 64 * c + 32 * h
                        src = bass.AP(x_dram.tensor, base + HALF * c * ROW,
                                      [[ROW, FIELDS], [STEP * ROW, ROT], [1, N]])
                        sp.dma_start(xrot[g:g + 32, s, :, :], src).then_inc(x_in[s], 16)
                for c in range(2):
                    d = U[c, 1] - U[c, 0]
                    src = bass.AP(x_dram.tensor, base + U[c, 0] * ROW,
                                  [[d * ROW, 2], [ROW, FIELDS], [1, N]])
                    sp.dma_start(xoth[64 * c:64 * c + 64, s, :], src).then_inc(x_in[s], 16)

            def load_quad(k):
                for a in range(2):
                    for dst, field in ((xlow, 0), (xhigh, HALF)):
                        src = bass.AP(x_dram.tensor, x_dram.offset + (k * TPB + 2 * a) * N + field * ROW,
                                      [[ROW, 2 * LEFT], [N, 2], [1, N]])
                        sp.dma_start(dst[64 * a:64 * a + 64, :], src).then_inc(quad_in, 16)

            def rotate_hidden(t, s):
                sp.wait_ge(hid_ready, 2 * t + 2)
                for i in range(1, ROT):
                    for c in range(2):
                        sp.dma_start(hid[HID * c:HID * (c + 1), s, i, :],
                                     hid[i:i + HID, s, 0, :]).then_inc(hid_in[s][i], 16)

            sp.dma_start(dn[:], dense.rearrange("(q p) c -> p q c", p=P)).then_inc(top_in, 16)
            sp.dma_start(wA[64:128, 0, :], W_top1[0:HID, :]).then_inc(top_in, 16)
            sp.wait_ge(zeroed, 3)
            sp.dma_start(wA[0:DENSE, 0, :], W_top1[HID + OUT:HID + OUT + DENSE, :]).then_inc(top_in, 16)
            sp.dma_start(wA[:, 1, :], W_top1[HID:HID + OUT, :]).then_inc(top_in, 16)
            sp.dma_start(wB, W_top2.rearrange("(m p) n -> p m n", p=P)).then_inc(top_in, 16)
            with nc.allow_non_contiguous_dma(reason="a few hundred bias and weight values"):
                sp.dma_start(wC[:], W_top3.rearrange("(m p) a -> p (m a)", p=P)).then_inc(top_in, 16)
                sp.dma_start(biasA[:], b_top1.rearrange("(m p) -> p m", p=P)).then_inc(top_in, 16)
                sp.dma_start(biasB[:], b_top2.rearrange("(m p) -> p m", p=P)).then_inc(top_in, 16)
            def write_first(n, a, b):
                for copy in range(2):
                    dst = bass.AP(x_dram.tensor, x_dram.offset + (copy * FIELDS + n * GROUP) * ROW + a * DIM,
                                  [[DIM, b - a], [ROW, GROUP], [1, DIM]])
                    sp.dma_start(dst, rows[a:b, n * GROUP:(n + 1) * GROUP, :]).then_inc(x_first, 16)

            for n, done in enumerate(gathered):
                sp.wait_ge(done, 16 * GROUP)
                write_first(n, 0, FIRST if n == len(gathered) - 1 else P)
            sp.wait_ge(x_first, 32 * len(gathered))
            sp.wait_ge(w0_folded, 9)
            load_x(0, 0)
            load_quad(0)
            load_x(1, 1)
            sp.wait_ge(top_high, 2)
            sp.wait_ge(top_low, 2)
            load_x(2, 2)
            load_x(3, 3)
            rotate_hidden(0, 0)
            write_first(len(gathered) - 1, FIRST, P)
            sp.wait_ge(x_first, X_FIRST)

            def body(k, more):
                for q in range(TPB):
                    t = k * TPB + q
                    if more or q < TPB - 1:
                        rotate_hidden(t + 1, (q + 1) % 2)
                    if more and q == 0:
                        sp.wait_ge(quad_made, k + 1)
                        load_quad(k + 1)
                    if more:
                        sp.wait_ge(z1_ready, (t + 1) * 2)
                        load_x(t + TPB, q)

            BPG = BODIES // GT
            for k in range(BPG - 1):
                body(k, True)
            with sp.Fori(1, GT) as g:
                sp.wait_ge(x_written, g * (32 * len(gathered)))
                for j in range(BPG):
                    body(g * BPG + (j - 1), True)
            body(BODIES - 1, False)
            sp.wait_ge(y_ready, B // N)
            sp.dma_start(out.rearrange("b a -> a b"), yrow[0:1, :]).then_inc(y_out, 16)
            sp.wait_ge(y_out, 16)

        @block.scalar
        def _(act):
            for i in range(ROT):
                act.wait_ge(w_turned, i + 1)
                bank = weight_banks[i + 2].rearrange("p (a b) -> p a b", a=ROT)
                nc.scalar.activation(w1T[:, i - 1, :, :] if i else wsh[:], bank, ACT.Copy).then_inc(w_high, 1)
            act.wait_ge(w_turned, ROT + 1)
            nc.scalar.activation(w0h[:], weight_banks[0].rearrange("p (a b) -> p a b", a=ROT),
                                 ACT.Copy).then_inc(w_high, 1)
            act.wait_ge(w_turned, ROT + 2)
            nc.scalar.activation(wp[:], weight_banks[1][:, 0:2 * OUT].rearrange("p (a b) -> p a b", a=2),
                                 ACT.Copy).then_inc(w_high, 1)
            act.wait_ge(w_in, 64)
            act.wait_ge(zeroed, 3)
            act.wait_ge(top_in, 8 * 16)
            act.wait_ge(dense_turned, 1)
            nc.scalar.activation(sum0[0:DENSE, :], pt[0:DENSE, 0:B // N, :].rearrange("p a b -> p (a b)"),
                                 ACT.Copy).then_inc(dense_ready, 1)
            nc.scalar.activation(wAh[:], wA, ACT.Copy).then_inc(top_high, 1)
            nc.scalar.activation(wBh[:], wB, ACT.Copy).then_inc(top_high, 1)

            def hidden_out(t, s):
                act.wait_ge(l0_done, t + 1)
                at_least(act, z1_ready, (t - 1) * 2)
                for c in range(2):
                    nc.scalar.activation(hid[64 * c:64 * c + 64, s, 0, :], y0[0:HID, s, :], ACT.Relu,
                                         bias=bias0[0:HID, :]).then_inc(hid_ready, 1)

            def direct_out(t, s):
                for a in range(SPT):
                    part = y0[HID:OUT, s, a * DIM:(a + 1) * DIM]
                    nc.scalar.activation(part, part, ACT.Relu, bias=bias0[HID:OUT, :],
                                         accum_out=sum0[HID:OUT, bass.ds(t * SPT + a, 1)]).then_inc(direct_summed, 1)

            def layer1_out(t, s):
                act.wait_ge(l1_blocks, (t + 1) * ROT)
                for a in range(SPT):
                    part = y1[:, s, a * DIM:(a + 1) * DIM]
                    nc.scalar.activation(part, part, ACT.Relu, bias=bias1[:],
                                         accum_out=sum1[:, bass.ds(t * SPT + a, 1)]).then_inc(last_summed, 1)

            def round0(t, s):
                act.wait_ge(z0_made, t + 1)
                at_least(act, l0_done, t - 1)
                nc.scalar.activation(z0h[:, s, :, :], z0[:], ACT.Copy).then_inc(z0_high, 1)

            def round_quad(k):
                act.wait_ge(quad_made, k + 1)
                at_least(act, pair_ready, 4 * k)
                nc.scalar.activation(zql[:], zq[:], ACT.Copy).then_inc(quad_high, 1)

            def stack_pair(k, a):
                act.wait_ge(quad_low, k + 1)
                at_least(act, l0_done, k * TPB + 2 * a)
                mine = slice(64 * a, 64 * a + 64)
                nc.scalar.activation(zps[0:64, :], zq[mine, :], ACT.Copy).then_inc(pair_ready, 1)
                nc.scalar.activation(zps[64:128, :], zql[mine, :].bitcast(F32), ACT.Copy).then_inc(pair_ready, 1)

            def round_split(t):
                act.wait_ge(zs_made, t + 1)
                at_least(act, l1_blocks, (t - 1) * ROT + ORDER1.index(0) + 1)
                nc.scalar.activation(zsh[:], zs[:], ACT.Copy).then_inc(zs_high, 1)

            def round_sums(b):
                if b:
                    act.wait_ge(l0_done, TILES)
                act.wait_ge(direct_summed, (b + 1) * N)
                act.wait_ge(last_summed, (b + 1) * N)
                nc.scalar.activation(sum_halves[b][:, 0, :, :], sums[:, :, b * N:(b + 1) * N],
                                     ACT.Copy).then_inc(sum_high, 1)

            def body(k, first, more):
                for q in range(TPB):
                    t = k * TPB + q
                    if more or q < TPB - 1:
                        hidden_out(t + 1, (q + 1) % 2)
                    if q == 0:
                        stack_pair(k, 1)
                    elif q == 2 and more:
                        stack_pair(k + 1, 0)
                    if more or q < TPB - 1:
                        direct_out(t + 1, (q + 1) % 2)
                    if q == 1 and more:
                        round_quad(k + 1)
                    if not (first and q == 0):
                        layer1_out(t - 1, (q + 1) % 2)
                    if more or q < TPB - 1:
                        round_split(t + 1)
                    if more or q < 1:
                        round0(t + 3, (q + 1) % 2)

            act.wait_ge(half_made, 1)
            nc.scalar.activation(z0h[:, 0, 0:2, :], z0[:, 0:2, :], ACT.Copy).then_inc(half_high, 1)
            act.wait_ge(z0_made, 1)
            nc.scalar.activation(z0h[:, 0, 2:, :], z0[:, 2:, :], ACT.Copy).then_inc(z0_high, 1)
            round_quad(0)
            stack_pair(0, 0)
            hidden_out(0, 0)
            round0(1, 1)
            direct_out(0, 0)
            round_split(0)
            round0(2, 0)
            body(0, True, True)
            with act.Fori(1, BODIES - 1) as k:
                body(k, False, True)
            round_sums(0)
            body(BODIES - 1, False, False)
            layer1_out(TILES - 1, (TILES - 1) % 2)

            round_sums(1)
            for b in range(2):
                for m in range(M1):
                    act.wait_ge(hA_mm, M1 * b + m + 1)
                    nc.scalar.activation(hAh[b][m], pt[:, m, :], ACT.Relu,
                                         bias=biasA[:, m:m + 1]).then_inc(hA_high, 1)
                    nc.scalar.activation(hA[m][:, b, :], pt[:, m, :], ACT.Relu,
                                         bias=biasA[:, m:m + 1]).then_inc(hA_ready, 1)
            for b in range(2):
                for m in range(M2):
                    act.wait_ge(hB_mm, M2 * b + m + 1)
                    nc.scalar.activation(hB[m][:, b, :], y0[:, b, :] if m == 0 else y1[:, b, :], ACT.Relu,
                                         bias=biasB[:, m:m + 1]).then_inc(hB_ready, 1)
            for b in range(B // N):
                act.wait_ge(y_mm, b + 1)
                nc.scalar.activation(yrow[0:1, b * N:(b + 1) * N], pt[0:1, b, :], ACT.Copy).then_inc(y_ready, 1)

        @block.vector
        def _(dve):
            nc.vector.memset(sum0, 0.0).then_inc(zeroed, 1)
            nc.vector.memset(wA[0:64, 0, :], 0.0).then_inc(zeroed, 1)
            nc.vector.memset(fold[:, ROT:, :], 0.0).then_inc(zeroed, 1)
            dve.wait_ge(w_in, 64)
            w0v = w0n.rearrange("p (h f) -> p h f", h=FIELDS)
            w0dv = w0d.rearrange("p (h f) -> p h f", h=W2)
            for a in range(2):
                for b in range(2):
                    nc.vector.tensor_copy(w0dv[:, FIELDS * a:FIELDS * (a + 1), FIELDS * b:FIELDS * (b + 1)],
                                          w0v).then_inc(w0_repeated, 1)
            w1v = w1n.rearrange("p (h f) -> p h f", h=HID)
            w1dv = w1d.rearrange("p (h f) -> p h f", f=W2)
            for b in range(2):
                nc.vector.tensor_copy(w1dv[:, 0:HID, FIELDS * b:FIELDS * (b + 1)], w1v).then_inc(w1_repeated, 1)
                nc.vector.tensor_copy(w1dv[:, HID:HID + ROT, FIELDS * b:FIELDS * (b + 1)],
                                      w1v[:, 0:ROT, :]).then_inc(w1_repeated, 1)
            dve.wait_ge(w1_repeated, 4)
            for i in range(ROT):
                for c in range(2):
                    nc.vector.tensor_copy(
                        walks[:, i, :, 64 * c:64 * c + 64].rearrange("p j (h q) -> p j h q", h=2),
                        view(w1d, i * W2 + HALF * c,
                             [[STEP, ROT], [FIELDS * W2, 2], [W2 + 1, FIELDS]])).then_inc(w1_walked, 1)
            dve.wait_ge(w0_repeated, 4)
            dve.wait_ge(zeroed, 3)
            for c in range(2):
                for h in range(2):
                    u = U[c, h]
                    nc.vector.tensor_tensor(
                        fold[:, 0:ROT, 64 * c + 32 * h:64 * c + 32 * h + 32],
                        view(w0d, HALF * c * W2 + u, [[STEP * W2, ROT], [W2 + 1, FIELDS]]),
                        view(w0d, u * W2 + HALF * c, [[STEP, ROT], [W2 + 1, FIELDS]]),
                        ALU.add).then_inc(w0_folded, 1)
            for b in range(2):
                for both in range(2):
                    dst = fold[:, ROT + b, :].rearrange("p (c r b) -> p c r b", b=2, r=LEFT)[:, :, :, b]
                    src = view(w0d, HALF * (W2 if both else 1), [[0, 4], [W2 + 1, LEFT]])
                    if both:
                        dve.wait_ge(w0_folded, 5 + 2 * b)
                        nc.vector.tensor_tensor(dst, dst, src, ALU.add).then_inc(w0_folded, 1)
                    else:
                        nc.vector.tensor_copy(dst, src).then_inc(w0_folded, 1)
            dve.wait_ge(w0_folded, 8)
            nc.vector.tensor_copy(fold[:, 0, 0:FIELDS], view(w0d, 0, [[W2 + 1, FIELDS]])).then_inc(w0_folded, 1)

            dve.wait_ge(w_high, ROT + 2)
            nc.vector.tensor_tensor(wsl[:], weight_banks[2].rearrange("p (a b) -> p a b", a=ROT),
                                    wsh[:].bitcast(F32), ALU.subtract).then_inc(w_low, 1)
            nc.vector.tensor_tensor(w0l[:], weight_banks[0].rearrange("p (a b) -> p a b", a=ROT),
                                    w0h[:].bitcast(F32), ALU.subtract).then_inc(w_low, 1)
            for r in (32, 96):
                nc.vector.tensor_tensor(wp[r:r + 32, :, :],
                                        weight_banks[1][r:r + 32, 0:2 * OUT].rearrange("p (a b) -> p a b", a=2),
                                        wp[r:r + 32, :, :].bitcast(F32), ALU.subtract).then_inc(w_low, 1)

            dve.wait_ge(top_high, 2)
            nc.vector.tensor_tensor(wAl[:], wA, wAh[:].bitcast(F32), ALU.subtract).then_inc(top_low, 1)
            nc.vector.tensor_tensor(wBl[:], wB, wBh[:].bitcast(F32), ALU.subtract).then_inc(top_low, 1)

            def low_sums(b):
                dve.wait_ge(sum_high, b + 1)
                nc.vector.tensor_tensor(sum_halves[b][:, 1, :, :], sums[:, :, b * N:(b + 1) * N],
                                        sum_halves[b][:, 0, :, :].bitcast(F32), ALU.subtract).then_inc(sum_low, 1)

            def products0(t, s):
                dve.wait_ge(x_in[s], (t - s) * (4 * X_LOADS) + 16 * X_LOADS)
                at_least(dve, z0_low, t)
                nc.vector.tensor_tensor(z0[:], xoth[:, s:s + 1, :].to_broadcast([P, ROT, N]),
                                        xrot[:, s, :, :], ALU.mult).then_inc(z0_made, 1)

            def products_quad(k):
                dve.wait_ge(quad_in, k * (16 * QUAD_LOADS) + 16 * QUAD_LOADS)
                at_least(dve, pair_ready, 4 * k)
                nc.vector.tensor_tensor(zq[:], xlow[:], xhigh[:], ALU.mult).then_inc(quad_made, 1)

            def low0(t, s):
                dve.wait_ge(z0_high, t + 1)
                at_least(dve, l0_done, t)
                nc.vector.tensor_tensor(z0l[:], z0[:], z0h[:, s, :, :].bitcast(F32),
                                        ALU.subtract).then_inc(z0_low, 1)

            def low_quad(k):
                dve.wait_ge(quad_high, k + 1)
                nc.vector.tensor_tensor(zql[:], zq[:], zql[:].bitcast(F32), ALU.subtract).then_inc(quad_low, 1)

            def products1(i, t, s, xs):
                if i == 0:
                    dve.wait_ge(hid_ready, 2 * t + 2)
                    at_least(dve, zs_low, t)
                else:
                    dve.wait_ge(hid_in[s][i], (t - s) * 16 + 32)
                    at_least(dve, l1_blocks, (t - 1) * ROT + (ORDER1.index(i) + 1))
                nc.vector.tensor_tensor(zs[:] if i == 0 else z1[:, i - 1, :, :],
                                        hid[:, s, i:i + 1, :].to_broadcast([P, ROT, N]),
                                        xrot[:, xs, :, :], ALU.mult).then_inc(zs_made if i == 0 else z1_ready, 1)

            def products1_rest(t, s, xs):
                for i in (2, 3):
                    dve.wait_ge(hid_in[s][i], (t - s) * 16 + 32)
                at_least(dve, l1_blocks, t * ROT)
                nc.vector.tensor_tensor(z1[:, 1:3, :, :],
                                        view(hid[:, s, 2:4, :], 0, [[N, 2], [0, ROT], [1, N]]),
                                        view(xrot[:, xs, :, :], 0, [[0, 2], [N, ROT], [1, N]]),
                                        ALU.mult).then_inc(z1_ready, 1)

            def low_split(t):
                dve.wait_ge(zs_high, t + 1)
                at_least(dve, l1_blocks, (t - 1) * ROT + ORDER1.index(0) + 1)
                nc.vector.tensor_tensor(zsl[:], zs[:], zsh[:].bitcast(F32),
                                        ALU.subtract).then_inc(zs_low, 1)

            def body(k, first, more):
                for q in range(TPB):
                    t = k * TPB + q
                    at = (t, q % 2, q)
                    ahead = more or q < 2
                    products1(0, *at)
                    if first and q == 0:
                        low0(1, 1)
                    products1(1, *at)
                    low_split(t)
                    if ahead:
                        products0(t + 2, (q + 2) % TPB)
                    if more and q == 1:
                        products_quad(k + 1)
                    products1_rest(*at)
                    if ahead:
                        low0(t + 2, q % 2)
                    if more and q == 1:
                        low_quad(k + 1)

            dve.wait_ge(x_in[0], 16 * X_LOADS)
            for part, done in ((slice(0, 2), half_made), (slice(2, ROT), z0_made)):
                nc.vector.tensor_tensor(z0[:, part, :], xoth[:, 0:1, :].to_broadcast([P, 2, N]),
                                        xrot[:, 0, part, :], ALU.mult).then_inc(done, 1)
            products_quad(0)
            for part, high, done in ((slice(0, 2), half_high, half_low), (slice(2, ROT), z0_high, z0_low)):
                dve.wait_ge(high, 1)
                nc.vector.tensor_tensor(z0l[:, part, :], z0[:, part, :], z0h[:, 0, part, :].bitcast(F32),
                                        ALU.subtract).then_inc(done, 1)
            low_quad(0)
            products0(1, 1)
            dve.wait_ge(w_turned, ROT + 2)
            body(0, True, True)
            with dve.Fori(1, BODIES - 1) as k:
                body(k, False, True)
            body(BODIES - 1, False, False)
            low_sums(0)
            low_sums(1)
            for b in range(2):
                for m in range(M1):
                    dve.wait_ge(hA_ready, M1 * b + m + 1)
                    nc.vector.tensor_tensor(hAl[b][m], hA[m][:, b, :], hAh[b][m].bitcast(F32),
                                            ALU.subtract).then_inc(hA_low, 1)

        @block.tensor
        def _(pe):
            pe.wait_ge(ident_ready, 1)
            pe.wait_ge(w1_walked, 2 * ROT)
            for i in range(ROT):
                for j in range(ROT):
                    turned = nc.tensor.transpose(weight_banks[i + 2][:, j * OUT:(j + 1) * OUT],
                                                 walks[:, i, j, :], ident[:])
                turned.then_inc(w_turned, 1)
            pe.wait_ge(w0_folded, 9)
            for j in range(ROT):
                turned = nc.tensor.transpose(weight_banks[0][:, j * OUT:(j + 1) * OUT], fold[:, j, :], ident[:])
            turned.then_inc(w_turned, 1)
            for b in range(2):
                turned = nc.tensor.transpose(weight_banks[1][:, b * OUT:(b + 1) * OUT], fold[:, ROT + b, :], ident[:])
            turned.then_inc(w_turned, 1)
            pe.wait_ge(top_in, 8 * 16)
            for q in range(B // P):
                turned = nc.tensor.transpose(pt[0:DENSE, q // 4, (q % 4) * P:(q % 4 + 1) * P], dn[:, q, :], ident[:])
            turned.then_inc(dense_turned, 1)
            pe.wait_ge(w_low, 4)

            def layer0(t, s):
                at_least(pe, direct_summed, (t - 1) * SPT)
                halves = isinstance(t, int) and t == 0
                for j in range(ROT):
                    if halves and j < 2:
                        pe.wait_ge(half_high, 1)
                    else:
                        pe.wait_ge(z0_high, t + 1)
                    for w in (w0h, w0l):
                        nc.tensor.matmul(y0[:, s, :], w[:, j, :], z0h[:, s, j, :], start=(j == 0 and w is w0h),
                                         stop=False)
                for j in range(ROT):
                    if halves and j < 2:
                        pe.wait_ge(half_low, 1)
                    else:
                        pe.wait_ge(z0_low, t + 1)
                    nc.tensor.matmul(y0[:, s, :], w0h[:, j, :], z0l[:, j, :], start=False, stop=False)
                pe.wait_ge(pair_ready, (t - s) + 2)
                nc.tensor.matmul(y0[:, s, :], wp[:, s, :], zps[:], start=False, stop=True).then_inc(l0_done, 1)

            def layer1(t, s):
                at_least(pe, last_summed, (t - 1) * SPT)
                for i in ORDER1:
                    if i == 0:
                        pe.wait_ge(zs_high, t + 1)
                        for j in range(ROT):
                            for w in (wsh, wsl):
                                nc.tensor.matmul(y1[:, s, :], w[:, j, :], zsh[:, j, :], start=False, stop=False)
                        pe.wait_ge(zs_low, t + 1)
                        for j in range(ROT):
                            mm = nc.tensor.matmul(y1[:, s, :], wsh[:, j, :], zsl[:, j, :], start=False, stop=False)
                    else:
                        pe.wait_ge(z1_ready, t * 2 + min(i, 2))
                        for j in range(ROT):
                            mm = nc.tensor.matmul(y1[:, s, :], w1T[:, i - 1, j, :], z1[:, i - 1, j, :],
                                                  start=(i == ORDER1[0] and j == 0),
                                                  stop=(i == ORDER1[-1] and j == ROT - 1))
                    mm.then_inc(l1_blocks, 1)

            def body(k, more):
                for q in range(TPB):
                    t = k * TPB + q
                    if more or q < TPB - 1:
                        layer0(t + 1, (q + 1) % 2)
                    layer1(t, q % 2)

            layer0(0, 0)
            body(0, True)
            with pe.Fori(1, BODIES - 1) as k:
                body(k, True)
            body(BODIES - 1, False)

            for b in range(2):
                pe.wait_ge(sum_low, b + 1)
                for m in range(M1):
                    if b:
                        pe.wait_ge(hA_ready, m + 1)
                    units = slice(m * P, (m + 1) * P)
                    passes = [(w, sum_halves[b][:, part, a, :]) for part, ws in ((0, (wAh, wAl)), (1, (wAh,)))
                              for w in ws for a in range(2)]
                    for n, (w, z) in enumerate(passes):
                        mm = nc.tensor.matmul(pt[:, m, :], w[:, n % 2, units], z,
                                              start=(n == 0), stop=(n == len(passes) - 1))
                    mm.then_inc(hA_mm, 1)
            NB = B // N
            for b in range(2):
                pe.wait_ge(hA_low, M1 * b + M1)
                for m in range(M2):
                    dst = y0[:, b, :] if m == 0 else y1[:, b, :]
                    units = slice(m * P, (m + 1) * P)
                    passes = [(w, a, h[b][a]) for w, h in ((wBh, hAh), (wBl, hAh), (wBh, hAl)) for a in range(M1)]
                    for n, (w, a, z) in enumerate(passes):
                        mm = nc.tensor.matmul(dst, w[:, a, units], z, start=(n == 0), stop=(n == len(passes) - 1))
                    mm.then_inc(hB_mm, 1)
            for b in range(NB):
                pe.wait_ge(hB_ready, M2 * (b + 1))
                for m in range(M2):
                    mm = nc.tensor.matmul(pt[0:1, b, :], wC[:, m:m + 1], hB[m][:, b, :],
                                          start=(m == 0), stop=(m == M2 - 1))
                mm.then_inc(y_mm, 1)


_TABLES = [f"tbl_{f}" for f in range(FIELDS)]
_INS = ["dense_ctx", "ids"] + _TABLES + ["W_top1", "b_top1", "W_top2", "b_top2", "W_top3",
                                         "L0_rec_w0", "L0_rec_b0", "L0_rec_w1", "L0_rec_b1"]


def kernel(**inputs):
    import concourse.bacc as bacc
    from concourse.bass_utils import run_bass_kernel_spmd

    nc = bacc.Bacc("TRN2", target_bir_lowering=False, num_devices=1)
    arrays, aps = {}, {}
    for name in _INS:
        a = np.ascontiguousarray(inputs[name])
        arrays[f"in_{name}"] = a
        aps[name] = nc.dram_tensor(f"in_{name}", a.shape, mybir.dt.from_np(a.dtype), kind="ExternalInput").ap()
    out = nc.dram_tensor("out_y", (inputs["ids"].shape[0], 1), F32, kind="ExternalOutput").ap()
    build(nc, aps["dense_ctx"], aps["ids"], [aps[t] for t in _TABLES], aps["W_top1"], aps["b_top1"],
          aps["W_top2"], aps["b_top2"], aps["W_top3"], aps["L0_rec_w0"], aps["L0_rec_b0"],
          aps["L0_rec_w1"], aps["L0_rec_b1"], out)
    r = run_bass_kernel_spmd(nc, [arrays], core_ids=[0])
    return r.results[0]["out_y"]
```
